# Optimizing a Trainium2 kernel written in Bass

```python
import numpy as np
import jax
import jax.numpy as jnp

def _softmax(x, axis=-1):
    return jax.nn.softmax(x, axis=axis)

def _gelu(x):
    return jax.nn.gelu(x, approximate=True)

def _silu(x):
    return jax.nn.silu(x)

def _sigmoid(x):
    return jax.nn.sigmoid(x)

def _layernorm(x, axis=-1, eps=1e-05):
    m = jnp.mean(x, axis=axis, keepdims=True)
    v = jnp.var(x, axis=axis, keepdims=True)
    return (x - m) / jnp.sqrt(v + eps)

def _scatter_add(tgt, idx, src, axis=0):
    return tgt.at[idx].add(src)

def _segment_sum(src, seg, n):
    return jax.ops.segment_sum(src, seg, n)
kernel_name = 'mk_flamingo_gated_d1_seqx_r4_724227'

def setup_inputs(seed: int=0):
    np.random.seed(seed)
    _w = jnp.asarray

    def _rec_inputs():
        import jax
        import jax.numpy as jnp
        _rk = jax.random.key(seed)
        x = -0.000125 + 0.9999 * jax.random.normal(jax.random.fold_in(_rk, 1), (4, 512, 512), jnp.float32)
        _lenS = 512 - jax.random.randint(jax.random.fold_in(_rk, 7), (4,), 0, max(1, 512 // 4) + 1, jnp.int32)
        _lenS2 = 512 - jax.random.randint(jax.random.fold_in(_rk, 8), (4,), 0, max(1, 512 // 4) + 1, jnp.int32)
        itok_BxS_13_99985 = jax.random.randint(jax.random.fold_in(_rk, 11), (4, 512), 13, 99986, jnp.int32)
        _ctx_2048P = jax.random.normal(jax.random.fold_in(_rk, 12), (4, 16, 512), jnp.float32)
        _ctx_2048c = jax.random.dirichlet(jax.random.fold_in(_rk, 512), 0.3 * jnp.ones((16,), jnp.float32), (4, 512))
        _ctx_2048t = jnp.einsum('bsk,bkd->bsd', _ctx_2048c, _ctx_2048P)
        _ctx_2048t = _ctx_2048t * jax.lax.rsqrt(jnp.mean(jnp.square(_ctx_2048t)) + 1e-12) * 0.953939
        ctx_2048 = 6.82029e-06 + 0.0200006 * (_ctx_2048t + 0.3 * jax.random.normal(jax.random.fold_in(_rk, 612), (4, 512, 512), jnp.float32))
        _g = jax.random.normal(jax.random.fold_in(_rk, 9001), (2, 1), jnp.float32)
        _g = jnp.sign(_g) * jnp.maximum(jnp.abs(_g), 1.0) + (_g == 0) * 1.0
        g_xattn = _g[0]
        g_ffn = _g[1]
        return (x, itok_BxS_13_99985, ctx_2048, g_xattn, g_ffn)
    x, itok_BxS_13_99985, ctx_2048, g_xattn, g_ffn = _rec_inputs()

    def _L0_xattn_setup():
        import jax, jax.numpy as jnp
        import numpy as np
        B, S, D = (4, 1024, 512)
        E = 4
        F = 2048 // E
        VOCAB = 25000
        key = jax.random.key(seed)
        k1, k2, k3, k4, k5 = jax.random.split(key, 5)
        hidden_states = jax.random.normal(k1, (B, S, D), dtype=jnp.float32)
        token_ids = jax.random.randint(k2, (B, S), 0, VOCAB, dtype=jnp.int64)
        Wg = jax.random.normal(k3, (E, F, D), dtype=jnp.float32) * 0.02
        Wu = jax.random.normal(k4, (E, F, D), dtype=jnp.float32) * 0.02
        Wd = jax.random.normal(k5, (E, D, F), dtype=jnp.float32) * 0.02
        return {'hidden_states': hidden_states, 'token_ids': token_ids, 'Wg': Wg, 'Wu': Wu, 'Wd': Wd}
    _L0_xattn_all = _L0_xattn_setup()
    _L0_xattn_in = {k: v for k, v in _L0_xattn_all.items() if k in ()}
    del _L0_xattn_all

    def _L0_ffn_setup():
        import jax, jax.numpy as jnp
        import numpy as np
        E = 16
        K = 2
        D = 512
        I = 352
        CAP = 256
        VOCAB = 32320
        key = jax.random.key(seed)
        ks = jax.random.split(key, 11)
        B, S = (4, 256)
        sd = 1.0 / np.sqrt(D)
        si = 1.0 / np.sqrt(I)
        return {'x': jax.random.normal(ks[0], (B, S, D), jnp.float32), 'input_ids': jax.random.randint(ks[1], (B, S), 0, VOCAB, dtype=jnp.int64), 'gate_w': jax.random.normal(ks[2], (E, D), jnp.float32) * sd, 'gate_b': jax.random.normal(ks[3], (E,), jnp.float32) * 0.01, 'W1': jax.random.normal(ks[4], (E, I, D), jnp.float32) * sd, 'W3': jax.random.normal(ks[5], (E, I, D), jnp.float32) * sd, 'W2': jax.random.normal(ks[6], (E, D, I), jnp.float32) * si, 'Ws1': jax.random.normal(ks[7], (I, D), jnp.float32) * sd, 'Ws3': jax.random.normal(ks[8], (I, D), jnp.float32) * sd, 'Ws2': jax.random.normal(ks[9], (D, I), jnp.float32) * si}
    _L0_ffn_all = _L0_ffn_setup()
    _L0_ffn_in = {k: v for k, v in _L0_ffn_all.items() if k in ('input_ids', 'gate_w', 'gate_b', 'W1', 'W3', 'W2', 'Ws1', 'Ws3', 'Ws2')}
    del _L0_ffn_all
    return {'x': x, 'itok_BxS_13_99985': itok_BxS_13_99985, 'ctx_2048': ctx_2048, 'g_xattn': g_xattn, 'g_ffn': g_ffn, 'L0_ffn_input_ids': _L0_ffn_in['input_ids'], 'L0_ffn_gate_w': _L0_ffn_in['gate_w'], 'L0_ffn_gate_b': _L0_ffn_in['gate_b'], 'L0_ffn_W1': _L0_ffn_in['W1'], 'L0_ffn_W3': _L0_ffn_in['W3'], 'L0_ffn_W2': _L0_ffn_in['W2'], 'L0_ffn_Ws1': _L0_ffn_in['Ws1'], 'L0_ffn_Ws3': _L0_ffn_in['Ws3'], 'L0_ffn_Ws2': _L0_ffn_in['Ws2']}

def reference(x, itok_BxS_13_99985, ctx_2048, g_xattn, g_ffn, L0_ffn_input_ids, L0_ffn_gate_w, L0_ffn_gate_b, L0_ffn_W1, L0_ffn_W3, L0_ffn_W2, L0_ffn_Ws1, L0_ffn_Ws3, L0_ffn_Ws2):
    import jax
    import jax.numpy as jnp

    def _L0_xattn_ref(hidden_states, token_ids, Wg, Wu, Wd):
        import jax, jax.numpy as jnp
        import numpy as np
        B, S, D = (4, 1024, 512)
        E = 4
        F = 2048 // E
        VOCAB = 25000
        tokens_per_expert = VOCAB // E
        tid = jnp.clip(token_ids, 0, VOCAB - 1)
        expert_ids = jnp.minimum(tid // tokens_per_expert, E - 1)
        out = jnp.zeros_like(hidden_states)
        for e in range(E):
            g = jax.nn.silu(jnp.einsum('bsd,fd->bsf', hidden_states, Wg[e]))
            u = jnp.einsum('bsd,fd->bsf', hidden_states, Wu[e])
            y = jnp.einsum('bsf,df->bsd', g * u, Wd[e])
            out = jnp.where((expert_ids == e)[..., None], y, out)
        return out

    def _L0_ffn_ref(x, input_ids, gate_w, gate_b, W1, W3, W2, Ws1, Ws3, Ws2):
        import jax, jax.numpy as jnp
        import numpy as np
        E = 16
        K = 2
        D = 512
        I = 352
        CAP = 256
        VOCAB = 32320
        shape = x.shape
        xt = x.reshape(-1, D)
        T = xt.shape[0]
        logits = xt.astype(jnp.float32) @ gate_w.astype(jnp.float32).T
        scores = jnp.sqrt(jax.nn.softplus(logits))
        _, idx = jax.lax.top_k(scores + gate_b, K)
        w = jnp.take_along_axis(scores, idx, axis=1)
        w = w / jnp.sum(w, axis=1, keepdims=True)
        e = idx.reshape(-1)
        onehot = jax.nn.one_hot(e, E, dtype=jnp.int32)
        pos = jnp.sum(onehot * (jnp.cumsum(onehot, axis=0) - 1), axis=1)
        valid = pos < CAP
        posc = jnp.where(valid, pos, 0)
        x_pairs = jnp.repeat(xt, K, axis=0)
        x_pairs = jnp.where(valid[:, None], x_pairs, 0.0)
        buf = jnp.zeros((E, CAP, D), xt.dtype).at[e, posc].add(x_pairs)
        g = jnp.einsum('ecd,eid->eci', buf, W1).astype(jnp.float32)
        u = jnp.einsum('ecd,eid->eci', buf, W3).astype(jnp.float32)
        h = (jax.nn.silu(g) * u).astype(xt.dtype)
        out = jnp.einsum('eci,edi->ecd', h, W2)
        y_pairs = out[e, posc] * (w.reshape(-1) * valid)[:, None]
        y = y_pairs.reshape(T, K, D).sum(axis=1)
        gs = jax.nn.silu((xt @ Ws1.T).astype(jnp.float32))
        us = (xt @ Ws3.T).astype(jnp.float32)
        shared = (gs * us).astype(xt.dtype) @ Ws2.T
        return (y + shared).astype(x.dtype).reshape(shape)
    x = x + jnp.tanh(g_xattn[0]) * _L0_xattn_ref(_layernorm(x, axis=-1), itok_BxS_13_99985, ctx_2048, ctx_2048, ctx_2048)
    x = x + jnp.tanh(g_ffn[0]) * _L0_ffn_ref(_layernorm(x, axis=-1), L0_ffn_input_ids, L0_ffn_gate_w, L0_ffn_gate_b, L0_ffn_W1, L0_ffn_W3, L0_ffn_W2, L0_ffn_Ws1, L0_ffn_Ws3, L0_ffn_Ws2)
    return x

_drawn_inputs = setup_inputs


def setup_inputs(seed=0):
    import zlib

    import numpy as np

    out = dict(_drawn_inputs(seed))
    spreads = {}
    factors = {}
    for name, (base, spread) in spreads.items():
        noise = np.random.default_rng([zlib.crc32(name.encode()), seed]).standard_normal(out[name].shape)
        drawn = base * np.exp(spread * noise) if base else spread * noise
        out[name] = jnp.asarray(drawn.astype(out[name].dtype))
    for name, factor in factors.items():
        out[name] = (out[name] * factor).astype(out[name].dtype)
    return out
```

```python
import numpy as np
import concourse.bass as bass
from concourse import mybir
from contextlib import ExitStack

F32 = mybir.dt.float32
F32R = mybir.dt.float32r
I32 = mybir.dt.int32
ALU = mybir.AluOpType
ACT = mybir.ActivationFunctionType
AX = mybir.AxisListType

P = 128
TOK, D = 2048, 512
KD = D // P
NJ = TOK // P
E1, VOCAB1 = 4, 25000
NT = NJ + E1 - 1
E2, CAP = 16, 256
I_MLP = 352
NI = 3
IP = NI * P
LOG0 = I_MLP - 2 * P
TB = 4
NB = NJ // TB
BT = TB * P
NA = CAP // P
NQ = E2 * NA
EPS = 1e-5
PAD = TOK

C_ID, C_TRI, C_ONE, C_IOTA = 0, P, 2 * P, 3 * P
C_TOK = 4 * P
C_KEEP = C_TOK + NJ
C_EM = C_KEEP + E2 * NJ
C_SPARE = C_EM + E2
C_END = C_SPARE + NQ


def constants():
    c = np.zeros((P, C_END), np.float32)
    c[:, C_ID:C_ID + P] = np.eye(P)
    c[:, C_TRI:C_TRI + P] = np.triu(np.ones((P, P)), 1)
    c[:, C_ONE:C_ONE + P] = 1.0
    c[:, C_IOTA:C_IOTA + P] = np.arange(P)[None, :]
    c[:, C_TOK:C_TOK + NJ] = np.arange(TOK).reshape(P, NJ) - PAD
    c[:, C_KEEP:C_KEEP + E2 * NJ] = (np.arange(E2 * NJ) % NJ != 0)[None, :]
    c[:, C_EM:C_EM + E2] = np.arange(E2) - E2
    c[:, C_SPARE:C_SPARE + NQ] = np.arange(P)[:, None] + P * (np.arange(NQ) % NA)[None, :]
    return c



def gated_layer(nc, x, ids, ctx_t, gates, w13, w2, gate_b, const, out):
    stack = ExitStack()
    with stack:
        def sb(name, shape, dt=F32):
            return stack.enter_context(nc.sbuf_tensor(name, shape, dt))

        def sem(name):
            return stack.enter_context(nc.semaphore(name))

        xh = nc.dram_tensor("xh", (TOK, 2 * D), F32).ap()
        xh_rows = xh.rearrange("t (h d) -> (t h) d", h=2)
        xh_tiles = xh.rearrange("(p j) d -> j p d", j=NJ)
        out_tiles = out[0:TOK, :].rearrange("(p j) d -> j p d", j=NJ)

        PC = KD * IP
        assert PC == NI * D
        SW = 3 * PC
        CX = E1 * KD * D
        slot0 = sb("slot0", [P, 2 * SW], F32R)
        arena = sb("arena", [P, 2 * CX + 4 * KD * P], F32R)
        SLOT = [(slot0[:, 0:SW], slot0[:, SW:2 * SW]),
                (arena[:, 0:SW], arena[:, SW:2 * SW])]
        ctx_hi, ctx_lo = arena[:, 0:CX], arena[:, CX:2 * CX]
        hT = [arena[:, 2 * CX + n * KD * P:2 * CX + (n + 1) * KD * P] for n in range(2)]
        gT = [arena[:, 2 * CX + (2 + n) * KD * P:2 * CX + (3 + n) * KD * P] for n in range(2)]
        bl = sb("bl", [P, 2, KD, BT], F32R)
        hid = arena[:, 2 * SW:2 * SW + 4 * NI * BT].rearrange("p (r m n) -> p r m n", r=2, m=2)

        raw = sb("raw", [P, 3, PC])
        raw_flat = raw[:, :, :].rearrange("p a b -> p (a b)")
        cst = sb("cst", [P, C_END])
        ident, tri, ones = cst[:, C_ID:C_ID + P], cst[:, C_TRI:C_TRI + P], cst[:, C_ONE:C_ONE + P]
        iota = cst[:, C_IOTA:C_IOTA + P]
        tok_n = cst[:, C_TOK:C_TOK + NJ]
        gate_in = sb("gate_in", [P, 2])
        tg = sb("tg", [P, 2])
        tok_i = sb("tok_i", [P, NJ], I32)
        bias_b = sb("bias_b", [P, E2])
        small = sb("small", [P, 32 * NJ])
        big = [sb(f"big{n}", [P, NJ, E2]) for n in range(7)]
        qhot = sb("qhot", [P, 2, NJ, 2 * NQ])
        small_i = sb("small_i", [P, 6 * NJ], I32)
        cnt_i = sb("cnt_i", [P, 2, E1], I32)
        idx1 = sb("idx1", [P, NT, 2], I32)
        tile_e = sb("tile_e", [P, NT], I32)
        idx2 = sb("idx2", [P, NQ, 2], I32)
        w_slot = sb("w_slot", [P, NQ])
        cur = sb("cur", [P, 8], I32)
        front = sb("front", [P, 4, D])
        xa, h = front[:, 0:2, :], front[:, 2:4, :]
        xb = sb("xb", [P, 2, D])
        s_sb = sb("s_sb", [P, NI * CAP])
        gu = sb("gu", [P, NI * CAP])
        xh_sb = sb("xh_sb", [P, 2, 2 * D])
        stats = sb("stats", [P, 2, 6])
        mv = sb("mv", [P, 2, 2])
        nwt = sb("nwt", [P, 5, 2])
        ht = sb("ht", [P, 4, D])
        ys = sb("ys", [P, 2, D])
        log_sb = sb("log_sb", [P, BT])
        logits = sb("logits", [P, NJ, E2])
        zeros = log_sb
        onehot = [rows_[:, :, :].rearrange("p a (b n) -> p (a b) n", n=P) for rows_ in (front, ht)]

        def bank(name):
            return stack.enter_context(nc.psum_tensor(name, [P, 512], F32))
        psT = [bank(f"psT{n}") for n in range(2)]
        psG = [bank(f"psG{n}") for n in range(4)]
        psY = [bank(f"psY{n}") for n in range(2)]

        in_const, in_ids, in_gates, in_bias = (sem(n) for n in ("in_const", "in_ids", "in_gates", "in_bias"))
        raw_here = [sem(f"raw_here{c}") for c in range(3)]
        w_hi = [sem(f"w_hi{c}") for c in range(3)]
        w_lo = [sem(f"w_lo{c}") for c in range(3)]
        ctx_here = [sem(f"ctx_here{n}") for n in range(E1)]
        ctx_hi_done, ctx_lo_done = sem("ctx_hi_done"), sem("ctx_lo_done")
        tg_ready = sem("tg_ready")
        zeroed = sem("zeroed")
        spare_sent = sem("spare_sent")
        chain = sem("chain")
        r1_tot, r1_pre, r1_hot, r1_src, r1_idx = (sem(f"r1_{n}") for n in ("tot", "pre", "hot", "src", "idx"))
        r2_tot, r2_pre, r2_hot, r2_src, r2_idx = (sem(f"r2_{n}") for n in ("tot", "pre", "hot", "src", "idx"))
        xa_idx, xb_idx, xh_idx = sem("xa_idx"), sem("xb_idx"), sem("xh_idx")
        xa_here = [sem(f"xa_here{n}") for n in range(2)]
        xb_here = [sem(f"xb_here{n}") for n in range(2)]
        xh_sent = [sem(f"xh_sent{n}") for n in range(2)]
        stats_done, mv_done, newton, norm_ready = (sem(n) for n in ("stats_done", "mv_done", "newton", "norm_ready"))
        h_ready, hT_ps, hT_hi, hT_lo = (sem(n) for n in ("h_ready", "hT_ps", "hT_hi", "hT_lo"))
        p_ps, s_ready, gu_ready = (sem(n) for n in ("p_ps", "s_ready", "gu_ready"))
        gT_ps, gT_hi, gT_lo = (sem(n) for n in ("gT_ps", "gT_hi", "gT_lo"))
        y_ps, x1_ready, xh_ready = sem("y_ps"), sem("x1_ready"), sem("xh_ready")
        ht_here = [sem(f"ht_here{n}") for n in range(4)]
        x1_here = [sem(f"x1_here{n}") for n in range(2)]
        bT_ps, bT_hi, bT_lo = sem("bT_ps"), sem("bT_hi"), sem("bT_lo")
        up_ps, silu_ready, hid_ready, hid_hi, hid_lo = (
            sem(n) for n in ("up_ps", "silu_ready", "hid_ready", "hid_hi", "hid_lo"))
        log_copied, log_ps, log_ready = sem("log_copied"), sem("log_ps"), sem("log_ready")
        y2_ps, y2_copied, o_ready = sem("y2_ps"), sem("y2_copied"), sem("o_ready")
        out_sent = [sem(f"out_sent{n}") for n in range(2)]
        soft_in, soft = sem("soft_in"), sem("soft")
        g_idx, add_idx = sem("g_idx"), sem("add_idx")
        g_here = [sem(f"g_here{n}") for n in range(4)]
        g_ps, g_hi, g_lo = sem("g_ps"), sem("g_hi"), sem("g_lo")
        up3_ps, silu3, hid3, hid3_hi, hid3_lo = (sem(n) for n in ("up3_ps", "silu3", "hid3", "hid3_hi", "hid3_lo"))
        y3_ps, y3_ready = sem("y3_ps"), sem("y3_ready")
        added = [sem(f"added{n}") for n in range(2)]

        block = stack.enter_context(nc.Block())

        def as_f32(ap):
            return ap.bitcast(F32)

        def landed(q, par):
            return 8 * q + 8 * (2 - par)

        def chunks(ap):
            return ap.rearrange("p (k t) -> p k t", k=KD)

        FIRST, LOOP0, LOOP1, LAST = -2, 5, 17, NT + 2

        def stage1(eng, step):
            for t in range(FIRST, LOOP0):
                step(t, t % 2, t)
            with eng.Fori(0, (LOOP1 - LOOP0) // 2) as i:
                step(eng.snap(i * 2 + LOOP0), LOOP0 % 2, None)
                step(eng.snap(i * 2 + (LOOP0 + 1)), (LOOP0 + 1) % 2, None)
            for t in range(LOOP1, LAST):
                step(t, t % 2, t)

        def have(known, k):
            return known is None or 0 <= known + k < NT

        def had(known, k):
            return known is None or (known > FIRST and 0 <= known - 1 + k < NT)

        def stage3(eng, step):
            for e in range(3):
                step(e, e % 2, e)
            with eng.Fori(0, E2 // 2 - 2) as i:
                step(eng.snap(i * 2 + 3), 1, None)
                step(eng.snap(i * 2 + 4), 0, None)
            step(E2 - 1, (E2 - 1) % 2, E2 - 1)

        def ctx_raw(e):
            if e < 2:
                return raw_flat[:, e * KD * D:(e + 1) * KD * D]
            return (ht if e == 2 else xh_sb)[:, :, :].rearrange("p a d -> p (a d)")

        def piece(ap, c):
            return ap[:, c * PC:(c + 1) * PC]

        @block.sync
        def _(sp):
            def load(s, c, known=True):
                if not (known and isinstance(s, int) and s == 0):
                    sp.wait_ge(w_lo[c], s)
                src = (w13[bass.ds(s, 1), :, c, :] if c < 2 else w2[bass.ds(s, 1), :, :])
                sp.dma_start(raw[:, c, :], src.rearrange("a p n -> (a p) n")).then_inc(raw_here[c], 16)

            sp.dma_start(tok_i[:, :], ids).then_inc(in_ids, 16)
            sp.dma_start(cst[:, :], const).then_inc(in_const, 16)
            sp.dma_start(gate_in[:, :], gates).then_inc(in_gates, 16)
            sp.dma_start(bias_b[:, :], gate_b).then_inc(in_bias, 16)
            for e in range(E1):
                sp.dma_start(ctx_raw(e), ctx_t[e, :, :]).then_inc(ctx_here[e], 16)
            sp.wait_ge(zeroed, 1)
            for a in range(NA):
                sp.dma_start(out[TOK + a * P:TOK + (a + 1) * P, :], zeros[:, :]).then_inc(spare_sent, 16)
            sp.wait_ge(ctx_lo_done, E1)
            for c in range(3):
                load(0, c)
            for n in range(2):
                last = NT - 1 - (NT - 1 - n) % 2
                sp.wait_ge(xh_sent[n], landed(last, n))

            def load_ht(j):
                if j >= 4:
                    sp.wait_ge(bT_ps, j - 3)
                sp.dma_start(ht[:, j % 4, :], xh_tiles[j, :, D:2 * D]).then_inc(ht_here[j % 4], 16)

            for j in range(4):
                load_ht(j)
            for c in range(3):
                load(1, c)
            for j in range(4, NJ):
                load_ht(j)
            for c in range(2):
                load(2, c)

            def store(j):
                sp.wait_ge(o_ready, j + 1)
                sp.dma_start(out_tiles[j, :, :], xh_sb[:, j % 2, 0:D]).then_inc(out_sent[j % 2], 16)

            for j in range(NJ):
                if j >= 2:
                    sp.wait_ge(o_ready, j - 1)
                sp.dma_start(xb[:, j % 2, :], xh_tiles[j, :, 0:D]).then_inc(x1_here[j % 2], 16)
                if j >= 1:
                    store(j - 1)
            store(NJ - 1)
            with sp.Fori(2, E2) as s:
                load(sp.snap(s + 1), 0)
                load(sp.snap(s + 1), 1)
                load(s, 2)
            load(E2, 2)
            for a in range(NA):
                sp.wait_ge(added[a], 16 * E2)

        @block.gpsimd
        def _(pool):
            pool.memset(zeros[:, :], 0.0).then_inc(zeroed, 1)

            def index(n, table, q, col, done, count):
                pool.tensor_copy(cur[:, n:n + 1], table[:, bass.ds(q, 1), col]).then_inc(done, 1)
                pool.wait_ge(done, count)
                pool.nop(nofuse=True)
                return bass.IndirectOffsetOnAxis(ap=cur[:, n:n + 1], axis=0)

            pool.wait_ge(r1_idx, 1)
            for q in range(2):
                pool.indirect_dma_start(xa[:, q, :], None, x, index(q, idx1, q, 0, xa_idx, q + 1)).then_inc(xa_here[q], 16)

            def step(t, par, known):
                if have(known, 0):
                    if had(known, -1):
                        pool.wait_ge(x1_ready, t - 1)
                    i = index(2 + par, idx1, t, 0, xb_idx, t + 1)
                    pool.indirect_dma_start(xb[:, par, :], None, x, i).then_inc(xb_here[par], 16)
                if have(known, 4):
                    pool.wait_ge(h_ready, t + 3)
                    i = index(par, idx1, t + 4, 0, xa_idx, t + 5)
                    pool.indirect_dma_start(xa[:, par, :], None, x, i).then_inc(xa_here[par], 16)
                if have(known, -2):
                    pool.wait_ge(xh_ready, t - 1)
                    i = index(4 + par, idx1, t - 2, 1, xh_idx, t - 1)
                    pool.indirect_dma_start(xh, i, xh_sb[:, par, :], None,
                                            bounds_check=TOK - 1, oob_is_err=False).then_inc(xh_sent[par], 16)

            for t in range(FIRST, LOOP0):
                step(t, t % 2, t)
            with pool.Fori(0, (LOOP1 - LOOP0) // 2 - 1) as i:
                step(pool.snap(i * 2 + LOOP0), LOOP0 % 2, None)
                step(pool.snap(i * 2 + (LOOP0 + 1)), (LOOP0 + 1) % 2, None)
            for t in range(LOOP1 - 2, LAST):
                step(t, t % 2, t)

            for j in range(NJ):
                r = j % 2
                pool.wait_ge(x1_here[r], landed(j, r))
                pool.wait_ge(y2_copied, j + 1)
                if j >= 2:
                    pool.wait_ge(out_sent[r], landed(j - 2, r))
                pool.tensor_tensor(xh_sb[:, r, 0:D], ys[:, r, :], xb[:, r, :], ALU.add).then_inc(o_ready, 1)

            def gather(e, r, free):
                for a in range(NA):
                    n = 2 * r + a
                    if free:
                        pool.wait_ge(g_ps, (e - 2) * NA + a + 1)
                    i = index(n, idx2, e * NA + a, 0, g_idx, e * NA + a + 1)
                    pool.indirect_dma_start(ht[:, n, :], None, xh_rows, i).then_inc(g_here[n], 16)

            def add(e, first):
                for a in range(NA):
                    pool.wait_ge(y3_ready, e * NA + a + 1)
                    if not first and a == 0:
                        for b in range(NA):
                            pool.wait_ge(added[b], e * 16)
                    i = index(4 + a, idx2, e * NA + a, 1, add_idx, e * NA + a + 1)
                    pool.indirect_dma_start(out, i, ys[:, a, :], None,
                                            compute_op=ALU.add).then_inc(added[a], 16)

            pool.wait_ge(r2_idx, 1)
            gather(0, 0, False)
            gather(1, 1, False)
            pool.wait_ge(spare_sent, 16 * NA)
            for r in range(2):
                pool.wait_ge(out_sent[r], landed(NJ - 2 + r, r))
            gather(2, 0, True)
            gather(3, 1, True)
            add(0, True)
            with pool.Fori(0, E2 // 2 - 2) as i:
                add(pool.snap(i * 2 + 1), False)
                gather(pool.snap(i * 2 + 4), 0, True)
                add(pool.snap(i * 2 + 2), False)
                gather(pool.snap(i * 2 + 5), 1, True)
            for e in range(E2 - 3, E2):
                add(e, False)

        @block.scalar
        def _(act):
            act.wait_ge(in_gates, 16)
            act.activation(tg[:, :], gate_in[:, :], ACT.Tanh).then_inc(tg_ready, 1)
            for e in range(E1):
                act.wait_ge(ctx_here[e], 16)
                act.activation(ctx_hi[:, e * KD * D:(e + 1) * KD * D], ctx_raw(e), ACT.Copy).then_inc(ctx_hi_done, 1)

            def norm(dst, src, col, done):
                act.activation(dst, src, ACT.Identity, scale=nwt[:, 3, col:col + 1],
                               bias=nwt[:, 4, col:col + 1]).then_inc(done, 1)

            def step(t, par, known):
                if have(known, -1):
                    act.wait_ge(gT_ps, t)
                    act.activation(gT[0], psT[1][:, :], ACT.Copy).then_inc(gT_hi, 1)
                if have(known, 0):
                    act.wait_ge(p_ps, t + 1)
                    if had(known, 0):
                        act.wait_ge(gu_ready, t)
                    act.activation(s_sb[:, 0:D], psG[0][:, :], ACT.Silu).then_inc(s_ready, 1)
                if have(known, 1):
                    act.wait_ge(hT_ps, t + 2)
                    act.activation(hT[0], psT[0][:, :], ACT.Copy).then_inc(hT_hi, 1)
                act.wait_ge(norm_ready, t + 3)
                if have(known, 2):
                    if had(known, 1):
                        act.wait_ge(hT_ps, t + 1)
                    norm(h[:, par, :], xa[:, par, :], 0, h_ready)
                if have(known, -2):
                    norm(xh_sb[:, par, D:2 * D], xh_sb[:, par, 0:D], 1, xh_ready)
            stage1(act, step)

            def split(s, c, r):
                act.wait_ge(raw_here[c], 16 * s + 16)
                act.activation(piece(SLOT[r][0], c), raw[:, c, :], ACT.Copy).then_inc(w_hi[c], 1)

            for c in range(3):
                split(0, c, 0)

            def transposed(j):
                act.wait_ge(bT_ps, j + 1)
                act.activation(bl[:, 0, :, (j % TB) * P:(j % TB + 1) * P], chunks(psT[j % 2][:, :]),
                               ACT.Copy).then_inc(bT_hi, 1)

            def hidden(n):
                b, i = n // NI, n % NI
                c = ORDER[i]
                act.wait_ge(up_ps, n + 1)
                if n:
                    act.wait_ge(hid_ready, n)
                act.activation(s_sb[:, 0:BT], psG[2 * (n % 2)][:, :], ACT.Silu).then_inc(silu_ready, 1)
                if i == 0:
                    if b:
                        act.wait_ge(log_ps, b)
                    else:
                        act.wait_ge(spare_sent, 16 * NA)
                    act.activation(log_sb[:, :], psG[2 * (n % 2)][:, :], ACT.Copy).then_inc(log_copied, 1)
                act.wait_ge(hid_ready, n + 1)
                if i == 0 and b >= 2:
                    act.wait_ge(y2_ps, TB * (b - 1))
                act.activation(hid[:, b % 2, 0, c * BT:(c + 1) * BT], gu[:, 0:BT], ACT.Copy).then_inc(hid_hi, 1)

            def rows(j):
                act.wait_ge(y2_ps, j + 1)
                if j >= 2:
                    act.wait_ge(o_ready, j - 1)
                act.activation(ys[:, j % 2, :], psY[j % 2][:, :], ACT.Copy, scale=tg[:, 1:2]).then_inc(y2_copied, 1)

            def router(n, dst, src, f, **kw):
                act.wait_ge(soft_in, n)
                act.activation(dst[:, :, :], src[:, :, :], f, **kw).then_inc(soft, 1)

            for j in range(TB):
                transposed(j)
            for b in range(NB):
                for i in range(NI - (b == NB - 1)):
                    hidden(b * NI + i)
                if b + 1 < NB:
                    for j in range(TB * (b + 1), TB * (b + 2)):
                        transposed(j)
                if b == 0:
                    split(1, 0, 1)
                    split(1, 1, 1)
                elif b < NB - 1:
                    for j in range(TB * (b - 1), TB * b):
                        rows(j)
            router(1, big[1], big[0], ACT.Exp, scale=-1.0)
            router(2, big[3], big[2], ACT.Ln)
            router(3, big[5], big[3], ACT.Sqrt)
            hidden(NB * NI - 1)
            for j in range(TB * (NB - 2), NJ):
                rows(j)

            def gathered(e):
                for a in range(NA):
                    act.wait_ge(g_ps, e * NA + a + 1)
                    act.activation(bl[:, 0, :, a * P:(a + 1) * P], chunks(psT[a][:, :]), ACT.Copy).then_inc(g_hi, 1)

            def rows3(e, first):
                for a in range(NA):
                    act.wait_ge(y3_ps, e * NA + a + 1)
                    if not first:
                        act.wait_ge(added[a], e * 16)
                    act.activation(ys[:, a, :], psY[a][:, :], ACT.Copy,
                                   scale=w_slot[:, bass.ds(e * NA + a, 1)]).then_inc(y3_ready, 1)

            def step(e, r, known):
                more = known is None or known + 1 < E2

                def silu(c):
                    act.wait_ge(up3_ps, e * NI + c + 1)
                    if known != 0 and c == 0:
                        act.wait_ge(hid3, e * NI)
                    act.activation(s_sb[:, c * CAP:(c + 1) * CAP], psG[c][:, 0:CAP], ACT.Silu).then_inc(silu3, 1)

                def high(c):
                    act.wait_ge(hid3, e * NI + c + 1)
                    if known != 0 and c == 0:
                        act.wait_ge(y3_ps, e * NA - NA)
                    act.activation(hid[:, r, 0, c * CAP:(c + 1) * CAP], gu[:, c * CAP:(c + 1) * CAP],
                                   ACT.Copy).then_inc(hid3_hi, 1)
                if more:
                    split(e + 2, 0, r)
                silu(0)
                if more:
                    split(e + 2, 1, r)
                high(0)
                silu(1)
                if known != 0:
                    act.wait_ge(y3_ps, e * NA - NA)
                split(e + 1, 2, 1 - r)
                high(1)
                silu(2)
                if more:
                    gathered(e + 1)
                high(2)
                if known is None or known > 0:
                    rows3(e - 1, known == 1)
            gathered(0)
            stage3(act, step)
            rows3(E2 - 1, False)

        @block.vector
        def _(dve):
            links = [0]

            def link(ins):
                links[0] += 1
                ins.then_inc(chain, 1)
                dve.wait_ge(chain, links[0])

            def S(n, w=1):
                return small[:, n * NJ:(n + w) * NJ]

            def SI(n, w=1):
                return small_i[:, n * NJ:(n + w) * NJ]

            def over(ap, n):
                return ap.unsqueeze(2).to_broadcast([P, ap.shape[1], n])

            def along(ap, n):
                return ap.unsqueeze(1).to_broadcast([P, n, ap.shape[1]])

            def low_ctx(e):
                dve.wait_ge(ctx_hi_done, e + 1)
                c = slice(e * KD * D, (e + 1) * KD * D)
                dve.tensor_tensor(ctx_lo[:, c], ctx_raw(e), as_f32(ctx_hi[:, c]), ALU.subtract).then_inc(ctx_lo_done, 1)

            dve.wait_ge(in_ids, 16)
            link(dve.tensor_copy(S(0), tok_i[:, :]))
            for e in range(1, E1):
                link(dve.tensor_scalar(S(e), S(0), float(VOCAB1 // E1 * e), None, ALU.is_ge))
            link(dve.tensor_scalar(S(4), S(1), -1.0, 1.0, ALU.mult, ALU.add))
            link(dve.tensor_tensor(S(5, 2), S(1, 2), S(2, 2), ALU.subtract))
            link(dve.tensor_copy(S(7), S(3)))
            dve.wait_ge(in_const, 16)
            link(dve.tensor_tensor_scan(S(8, E1), cst[:, C_KEEP:C_KEEP + E1 * NJ], S(4, E1), 0.0, ALU.mult, ALU.add))
            run = S(8, E1).rearrange("p (e j) -> p e j", e=E1)
            dve.tensor_copy(S(12)[:, 0:E1], run[:, :, NJ - 1]).then_inc(r1_tot, 1)
            dve.wait_ge(r1_pre, 1)
            link(dve.tensor_scalar(cnt_i[:, 0, :], psY[0][:, E1:2 * E1], float(P - 1), None, ALU.add))
            link(dve.tensor_scalar(cnt_i[:, 1, :], cnt_i[:, 0, :], -P, None, ALU.bitwise_and))
            link(dve.tensor_copy(S(13)[:, 0:E1], cnt_i[:, 1, :]))
            link(dve.tensor_tensor_scan(S(14)[:, 0:E1], ones[:, 0:E1], S(13)[:, 0:E1], 0.0, ALU.mult, ALU.add))
            link(dve.tensor_tensor(S(15)[:, 0:E1], S(14)[:, 0:E1], S(13)[:, 0:E1], ALU.subtract))
            link(dve.tensor_tensor(S(16)[:, 0:E1], S(15)[:, 0:E1], psY[0][:, 0:E1], ALU.add))
            link(dve.tensor_tensor(S(17, E1).rearrange("p (e j) -> p e j", e=E1), run, over(S(16)[:, 0:E1], NJ), ALU.add))
            link(dve.tensor_tensor(S(21, E1), S(17, E1), S(4, E1), ALU.mult))
            link(dve.tensor_reduce(S(25), S(21, E1).rearrange("p (e j) -> p j e", e=E1), AX.X, ALU.add))
            link(dve.tensor_scalar(SI(0), S(25), -1.0, None, ALU.add))
            link(dve.tensor_scalar(SI(1), SI(0), P - 1, None, ALU.bitwise_and))
            link(dve.tensor_scalar(SI(2), SI(0), 7, None, ALU.arith_shift_right))
            link(dve.tensor_copy(S(26, 2), SI(1, 2)))
            dve.tensor_tensor(onehot[0], along(iota, NJ), over(S(26), P), ALU.is_equal)
            link(dve.tensor_tensor(qhot[:, 0, :, 0:NT], along(iota[:, 0:NT], NJ), over(S(27), NT), ALU.is_equal))
            dve.tensor_tensor(qhot[:, 0, :, NQ:NQ + NT], qhot[:, 0, :, 0:NT], over(tok_n, NT), ALU.mult).then_inc(r1_hot, 1)
            link(dve.tensor_scalar(S(28, 2)[:, 0:NT], iota[:, 0:NT], float(P), S(14)[:, 0:1], ALU.mult, ALU.is_ge))
            for e in range(1, E1 - 1):
                link(dve.tensor_scalar(S(30, 2)[:, 0:NT], iota[:, 0:NT], float(P), S(14)[:, e:e + 1], ALU.mult, ALU.is_ge))
                link(dve.tensor_tensor(S(28, 2)[:, 0:NT], S(28, 2)[:, 0:NT], S(30, 2)[:, 0:NT], ALU.add))
            link(dve.tensor_copy(tile_e[:, :], S(28, 2)[:, 0:NT]))
            low_ctx(0)
            dve.wait_ge(r1_src, 1)
            dve.tensor_scalar(idx1[:, :, 0], psY[1][:, 0:NT], float(PAD), float(TOK - 1), ALU.add, ALU.min)
            dve.tensor_scalar(idx1[:, :, 1], psY[1][:, 0:NT], float(PAD), None, ALU.add).then_inc(r1_idx, 1)

            low_ctx(1)
            low_ctx(2)
            dve.wait_ge(tg_ready, 1)

            NEWTON = 8

            def step(t, par, known):
                one, two = have(known, 2), have(known, -2)
                if two:
                    dve.wait_ge(y_ps, t - 1)
                    dve.wait_ge(xb_here[par], landed(t - 2, par))
                    if known == 2:
                        dve.wait_ge(ctx_lo_done, E1)
                    if known is None or known >= 4:
                        dve.wait_ge(xh_sent[par], landed(t - 4, par))
                    dve.scalar_tensor_tensor(xh_sb[:, par, 0:D], psY[0][:, :], tg[:, 0:1], xb[:, par, :],
                                             ALU.mult, ALU.add).then_inc(x1_ready, 1)
                def low_g():
                    if have(known, -1):
                        dve.wait_ge(gT_hi, t)
                        dve.tensor_tensor(gT[1], psT[1][:, :], as_f32(gT[0]), ALU.subtract).then_inc(gT_lo, 1)
                cs = slice(0 if one else 1, 2 if two else 1)
                i = None
                if one:
                    dve.wait_ge(xa_here[par], landed(t + 2, par))
                    i = dve.bn_stats(stats[:, 0, :], xa[:, par, :])
                if two:
                    dve.wait_ge(x1_ready, t - 1)
                    i = dve.bn_stats(stats[:, 1, :], xh_sb[:, par, 0:D])
                k = t + 2
                if not (one or two):
                    dve.tensor_copy(stats[:, 0, 0:1], cst[:, 0:1]).then_inc(norm_ready, 1)
                else:
                    i.then_inc(stats_done, 1)
                low_g()
                if one or two:
                    dve.wait_ge(stats_done, NORMS(k, known))
                    dve.nop(nofuse=True)
                    if one:
                        i = dve.bn_aggr(mv[:, 0, :], stats[:, 0, :])
                    if two:
                        i = dve.bn_aggr(mv[:, 1, :], stats[:, 1, :])
                    i.then_inc(mv_done, 1)
                    dve.wait_ge(mv_done, NORMS(k, known))
                    base = (NORMS(k, known) - 1) * NEWTON
                    n = [0]

                    def nw(ins):
                        n[0] += 1
                        ins.then_inc(newton, 1)
                        dve.wait_ge(newton, base + n[0])
                    V, Y, T, R, B = (nwt[:, m, cs] for m in range(5))
                    nw(dve.tensor_scalar(V, mv[:, cs, 1], EPS, 0.5, ALU.add, ALU.mult))
                    nw(dve.tensor_scalar(Y.bitcast(I32), V.bitcast(I32), -0.5, float(0x5f3759df - (1 << 22) - (1 << 31)),
                                         ALU.mult, ALU.add))
                    for m in range(3):
                        for c in range(cs.start, cs.stop):
                            i = dve.tensor_scalar(nwt[:, 2, c:c + 1], nwt[:, 1, c:c + 1], nwt[:, 1, c:c + 1],
                                                  nwt[:, 0, c:c + 1], ALU.mult, ALU.mult)
                        nw(i)
                        if m == 2:
                            if had(known, 2):
                                dve.wait_ge(h_ready, t + 2)
                            if had(known, -2):
                                dve.wait_ge(xh_ready, t - 2)
                        nw(dve.scalar_tensor_tensor(R if m == 2 else Y, T, -1.5, Y, ALU.add, ALU.mult))
                    assert n[0] == NEWTON
                    dve.scalar_tensor_tensor(B, mv[:, cs, 0], -1.0, R, ALU.mult, ALU.mult).then_inc(norm_ready, 1)
                if have(known, 0):
                    dve.wait_ge(s_ready, t + 1)
                    if had(known, 0):
                        dve.wait_ge(gT_ps, t)
                    dve.tensor_tensor(gu[:, 0:D], s_sb[:, 0:D], psG[0][:, :], ALU.mult).then_inc(gu_ready, 1)
                if known == FIRST:
                    low_ctx(3)
                if have(known, 1):
                    dve.wait_ge(hT_hi, t + 2)
                    dve.tensor_tensor(hT[1], psT[0][:, :], as_f32(hT[0]), ALU.subtract).then_inc(hT_lo, 1)

            def NORMS(k, known):
                return k + 1
            stage1(dve, step)

            def split(s, c, r):
                dve.wait_ge(w_hi[c], s + 1)
                dve.tensor_tensor(piece(SLOT[r][1], c), raw[:, c, :], as_f32(piece(SLOT[r][0], c)),
                                  ALU.subtract).then_inc(w_lo[c], 1)

            for c in range(3):
                split(0, c, 0)

            def transposed(j):
                dve.wait_ge(bT_hi, j + 1)
                s = slice((j % TB) * P, (j % TB + 1) * P)
                dve.tensor_tensor(bl[:, 1, :, s], chunks(psT[j % 2][:, :]), as_f32(bl[:, 0, :, s]),
                                  ALU.subtract).then_inc(bT_lo, 1)

            def hidden(n):
                b, c = n // NI, ORDER[n % NI]
                dve.wait_ge(silu_ready, n + 1)
                if n:
                    dve.wait_ge(hid_hi, n)
                    dve.wait_ge(hid_lo, n)
                dve.tensor_tensor(gu[:, 0:BT], s_sb[:, 0:BT], psG[2 * (n % 2) + 1][:, :], ALU.mult).then_inc(hid_ready, 1)
                dve.wait_ge(hid_hi, n + 1)
                s = slice(c * BT, (c + 1) * BT)
                dve.tensor_tensor(hid[:, b % 2, 1, s], gu[:, 0:BT], as_f32(hid[:, b % 2, 0, s]),
                                  ALU.subtract).then_inc(hid_lo, 1)

            def take_logits(b):
                dve.wait_ge(log_ps, b + 1)
                src = psY[1][:, :].rearrange("p (j n) -> p j n", j=TB)[:, :, LOG0:LOG0 + E2]
                dve.tensor_copy(logits[:, b * TB:(b + 1) * TB, :], src).then_inc(log_ready, 1)

            for j in range(TB):
                transposed(j)
            for b in range(NB):
                hidden(b * NI)
                hidden(b * NI + 1)
                take_logits(b)
                if b < NB - 1:
                    hidden(b * NI + 2)
                    for j in range(TB * (b + 1), TB * (b + 2)):
                        transposed(j)
                if b == 0:
                    split(1, 0, 1)
                    split(1, 1, 1)

            B = [x_[:, :, :] for x_ in big]
            L = logits[:, :, :]
            dve.wait_ge(log_ready, NB)
            dve.scalar_tensor_tensor(B[0], L, -1.0, L, ALU.mult, ALU.max).then_inc(soft_in, 1)
            dve.wait_ge(soft, 1)
            dve.tensor_scalar(B[2], B[1], 1.0, None, ALU.add).then_inc(soft_in, 1)
            dve.wait_ge(soft_in, 2)
            link(dve.tensor_scalar(B[4], B[2], -1.0, None, ALU.add))
            link(dve.tensor_scalar(B[0], B[4], 1e-30, None, ALU.max))
            link(dve.reciprocal(B[0], B[0]))
            link(dve.tensor_tensor(B[0], B[0], B[1], ALU.mult))
            link(dve.scalar_tensor_tensor(B[4], B[4], 0.0, B[1], ALU.is_equal, ALU.mult))
            link(dve.scalar_tensor_tensor(B[4], L, 0.0, B[4], ALU.max, ALU.add))
            dve.wait_ge(soft, 2)
            link(dve.tensor_tensor(B[6], B[3], B[0], ALU.mult))
            dve.tensor_tensor(B[3], B[6], B[4], ALU.add).then_inc(soft_in, 1)
            dve.wait_ge(soft, 3)
            dve.wait_ge(in_bias, 16)
            link(dve.tensor_tensor(B[0], B[5], along(bias_b[:, :], NJ), ALU.add))
            em = along(cst[:, C_EM:C_EM + E2], NJ)
            pick = [B[1], B[2]]
            for k in range(2):
                m, i = S(k), S(2 + k)
                link(dve.tensor_reduce(m, B[0], AX.X, ALU.max))
                link(dve.tensor_tensor(B[3], B[0], over(m, E2), ALU.is_equal))
                link(dve.tensor_tensor(B[3], B[3], em, ALU.mult))
                link(dve.tensor_reduce(i, B[3], AX.X, ALU.min))
                link(dve.tensor_tensor(pick[k], em, over(i, E2), ALU.is_equal))
                if k == 0:
                    link(dve.scalar_tensor_tensor(B[0], pick[0], -3e38, B[0], ALU.mult, ALU.add))
            by_e = B[3].rearrange("p j e -> p (j e)").rearrange("p (e j) -> p j e", e=E2)
            link(dve.tensor_tensor(by_e, pick[0], pick[1], ALU.add))
            flat = [b_.rearrange("p j e -> p (j e)") for b_ in B]
            link(dve.tensor_tensor_scan(flat[4], cst[:, C_KEEP:C_KEEP + E2 * NJ], flat[3], 0.0, ALU.mult, ALU.add))
            count = flat[4].rearrange("p (e j) -> p e j", e=E2)
            dve.tensor_copy(S(4), count[:, :, NJ - 1]).then_inc(r2_tot, 1)
            for k in range(2):
                link(dve.tensor_tensor(B[6], pick[k], B[5], ALU.mult))
                link(dve.tensor_reduce(S(5 + k), B[6], AX.X, ALU.add))
            link(dve.tensor_tensor(S(7), S(5), S(6), ALU.add))
            link(dve.reciprocal(S(7), S(7)))
            for k in range(2):
                link(dve.scalar_tensor_tensor(S(5 + k), S(5 + k), tg[:, 1:2], S(7), ALU.mult, ALU.mult))
            hidden(NB * NI - 1)
            dve.wait_ge(r2_pre, 1)
            link(dve.tensor_tensor(flat[0].rearrange("p (e j) -> p e j", e=E2), count, over(psG[0][:, 0:E2], NJ), ALU.add))
            pos = flat[0].rearrange("p (e j) -> p j e", e=E2)
            for k in range(2):
                link(dve.tensor_tensor(B[6], pick[k], pos, ALU.mult))
                link(dve.tensor_reduce(S(8 + k), B[6], AX.X, ALU.add))
            link(dve.scalar_tensor_tensor(S(10, 2), S(2, 2), float(CAP), S(8, 2), ALU.mult, ALU.add))
            link(dve.tensor_scalar(SI(0, 2), S(10, 2), float(E2 * CAP - 1), None, ALU.add))
            link(dve.tensor_scalar(SI(2, 2), SI(0, 2), P - 1, None, ALU.bitwise_and))
            link(dve.tensor_scalar(SI(4, 2), SI(0, 2), 7, None, ALU.arith_shift_right))
            link(dve.tensor_copy(S(12, 4), SI(2, 4)))
            link(dve.tensor_scalar(S(16, 2), S(8, 2), float(CAP), 1024.0, ALU.is_gt, ALU.mult))
            link(dve.tensor_tensor(S(14, 2), S(14, 2), S(16, 2), ALU.add))
            for k in range(2):
                dve.tensor_tensor(onehot[k], along(iota, NJ), over(S(12 + k), P), ALU.is_equal)
                q = qhot[:, k, :, :]
                link(dve.tensor_tensor(q[:, :, 0:NQ], along(iota[:, 0:NQ], NJ), over(S(14 + k), NQ), ALU.is_equal))
                link(dve.tensor_tensor(q[:, :, NQ:2 * NQ], q[:, :, 0:NQ], over(S(5 + k), NQ), ALU.mult))
                dve.tensor_tensor(q[:, :, 0:NQ], q[:, :, 0:NQ], over(tok_n, NQ), ALU.mult).then_inc(r2_hot, 1)
            dve.wait_ge(r2_src, 1)
            src = psG[1][:, 0:NQ]
            U = [S(18 + 2 * k, 2) for k in range(3)]
            link(dve.tensor_scalar(U[0], src, 0.0, None, ALU.is_equal))
            link(dve.tensor_scalar(U[1], src, 2.0, 2.0 * PAD + 1, ALU.mult, ALU.add))
            link(dve.tensor_tensor(U[2], U[0], cst[:, C_SPARE:C_SPARE + NQ], ALU.mult))
            link(dve.scalar_tensor_tensor(idx2[:, :, 0], U[0], -2.0 * PAD, U[1], ALU.mult, ALU.add))
            link(dve.scalar_tensor_tensor(idx2[:, :, 1], src, float(PAD), U[2], ALU.add, ALU.add))
            dve.tensor_copy(w_slot[:, :], psG[1][:, NQ:2 * NQ]).then_inc(r2_idx, 1)

            def gathered(e):
                for a in range(NA):
                    dve.wait_ge(g_hi, e * NA + a + 1)
                    s = slice(a * P, (a + 1) * P)
                    dve.tensor_tensor(bl[:, 1, :, s], chunks(psT[a][:, :]), as_f32(bl[:, 0, :, s]),
                                      ALU.subtract).then_inc(g_lo, 1)

            def step(e, r, known):
                more = known is None or known + 1 < E2

                def gate(c):
                    s = slice(c * CAP, (c + 1) * CAP)
                    dve.wait_ge(silu3, e * NI + c + 1)
                    if known != 0 and c == 0:
                        dve.wait_ge(hid3_lo, e * NI)
                    dve.tensor_tensor(gu[:, s], s_sb[:, s], psG[c][:, CAP:2 * CAP], ALU.mult).then_inc(hid3, 1)

                def low(c):
                    s = slice(c * CAP, (c + 1) * CAP)
                    dve.wait_ge(hid3_hi, e * NI + c + 1)
                    dve.tensor_tensor(hid[:, r, 1, s], gu[:, s], as_f32(hid[:, r, 0, s]), ALU.subtract).then_inc(hid3_lo, 1)
                if more:
                    split(e + 2, 0, r)
                gate(0)
                if more:
                    split(e + 2, 1, r)
                low(0)
                gate(1)
                split(e + 1, 2, 1 - r)
                low(1)
                gate(2)
                if more:
                    gathered(e + 1)
                low(2)
            gathered(0)
            stage3(dve, step)

        @block.tensor
        def _(pe):
            def product(ps, left, right, n, total):
                for m, (a, b) in enumerate(((0, 0), (0, 1), (1, 0))):
                    ins = pe.matmul(ps, left[a], right[b], start=n == 0 and m == 0, stop=n == total - 1 and m == 2)
                return ins

            def transpose4(ps, src):
                for k in range(KD):
                    ins = pe.transpose(ps[:, k * P:(k + 1) * P], src[:, k * P:(k + 1) * P], ident)
                return ins

            pe.wait_ge(in_const, 16)
            pe.wait_ge(r1_tot, 1)
            pe.matmul(psY[0][:, 0:E1], tri, S12(small)[:, 0:E1], start=True, stop=True)
            pe.matmul(psY[0][:, E1:2 * E1], ones, S12(small)[:, 0:E1], start=True, stop=True).then_inc(r1_pre, 1)
            pe.wait_ge(r1_hot, 1)
            for j in range(NJ):
                ins = pe.matmul(psY[1][:, 0:NT], onehot[0][:, j, :], qhot[:, 0, j, NQ:NQ + NT], start=j == 0, stop=j == NJ - 1)
            ins.then_inc(r1_src, 1)
            pe.wait_ge(r1_idx, 1)
            pe.nop(nofuse=True)

            def weights(t):
                return pe.value_load(tile_e[0:1, bass.ds(t, 1)], min_val=0, max_val=E1 - 1)

            def ctx(w, k):
                return [c[:, bass.ds(w * (KD * D) + k * D, D)] for c in (ctx_hi, ctx_lo)]

            def step(t, par, known):
                if have(known, 0):
                    w = weights(t)
                if have(known, -1):
                    v = weights(t - 1)
                    pe.wait_ge(gu_ready, t)
                    transpose4(psT[1], gu[:, 0:D]).then_inc(gT_ps, 1)
                if have(known, 0):
                    pe.wait_ge(hT_lo, t + 1)
                    pe.wait_ge(ctx_lo_done, pe.snap(w + 1))
                    for k in range(KD):
                        s = slice(k * P, (k + 1) * P)
                        ins = product(psG[0][:, :], [hT[0][:, s], hT[1][:, s]], ctx(w, k), k, KD)
                    ins.then_inc(p_ps, 1)
                if have(known, 1):
                    pe.wait_ge(h_ready, t + 2)
                    transpose4(psT[0], h[:, (par + 1) % 2, :]).then_inc(hT_ps, 1)
                if have(known, -1):
                    pe.wait_ge(gT_lo, t)
                    if have(known, -2):
                        pe.wait_ge(x1_ready, t - 1)
                    for k in range(KD):
                        s = slice(k * P, (k + 1) * P)
                        ins = product(psY[0][:, :], [gT[0][:, s], gT[1][:, s]], ctx(v, k), k, KD)
                    ins.then_inc(y_ps, 1)
            stage1(pe, step)

            def transposed(b):
                for j in range(TB * b, TB * (b + 1)):
                    pe.wait_ge(ht_here[j % 4], 16 * (j // 4 + 1))
                    if j >= 2:
                        pe.wait_ge(bT_lo, j - 1)
                    else:
                        pe.wait_ge(gT_lo, NT)
                    transpose4(psT[j % 2], ht[:, j % 4, :]).then_inc(bT_ps, 1)

            def up(b):
                pe.wait_ge(bT_lo, TB * (b + 1))
                for i, c in enumerate(ORDER):
                    n = b * NI + i
                    if n >= 2:
                        pe.wait_ge(hid_ready, n - 1)
                    if i == 2:
                        pe.wait_ge(log_copied, b + 1)
                    for m in range(2):
                        pe.wait_ge(w_lo[m], 1)
                        for k in range(KD):
                            o = k * IP + c * P
                            left = [piece(s, m)[:, o:o + P] for s in SLOT[0]]
                            ins = product(psG[2 * (n % 2) + m][:, :], left, [bl[:, 0, k, :], bl[:, 1, k, :]], k, KD)
                    ins.then_inc(up_ps, 1)
                    if i == 1:
                        pe.wait_ge(log_copied, b + 1)
                        if b >= 2:
                            pe.wait_ge(y2_copied, TB * (b - 1))
                        for j in range(TB):
                            s = slice(j * P, (j + 1) * P)
                            ins = pe.transpose(psY[1][:, s], log_sb[:, s], ident)
                        ins.then_inc(log_ps, 1)

            def down(b, extra=None):
                pe.wait_ge(hid_lo, NI * (b + 1))
                pe.wait_ge(w_lo[2], 1)
                for j in range(TB * b, TB * (b + 1)):
                    if j % TB == 1:
                        pe.wait_ge(log_ready, min(b + 2, NB))
                    if j >= 2:
                        pe.wait_ge(y2_copied, j - 1)
                    for c in range(NI):
                        o = c * BT + (j % TB) * P
                        left = [hid[:, b % 2, m, o:o + P] for m in range(2)]
                        right = [piece(s, 2)[:, c * D:(c + 1) * D] for s in SLOT[0]]
                        ins = product(psY[j % 2][:, :], left, right, c, NI)
                    ins.then_inc(y2_ps, 1)
                    if extra and j == extra[0]:
                        extra[1]()

            def totals():
                pe.wait_ge(r2_tot, 1)
                pe.matmul(psG[0][:, 0:E2], tri, small[:, 4 * NJ:5 * NJ], start=True, stop=True).then_inc(r2_pre, 1)

            transposed(0)
            for b in range(NB):
                up(b)
                if b + 1 < NB:
                    transposed(b + 1)
                if b >= 1:
                    down(b - 1)
            down(NB - 1, (TB * (NB - 1) + 1, totals))
            for k in range(2):
                pe.wait_ge(r2_hot, k + 1)
                for j in range(NJ):
                    ins = pe.matmul(psG[1][:, 0:2 * NQ], onehot[k][:, j, :], qhot[:, k, j, :],
                                    start=k == 0 and j == 0, stop=k == 1 and j == NJ - 1)
            ins.then_inc(r2_src, 1)

            def gathered(e, r, first):
                for a in range(NA):
                    n = 2 * r + a
                    pe.wait_ge(g_here[n], landed(e, r))
                    if not first:
                        pe.wait_ge(g_lo, (e - 1) * NA + a + 1)
                    transpose4(psT[a], ht[:, n, :]).then_inc(g_ps, 1)

            def down3(e, r, first):
                pe.wait_ge(hid3_lo, (e + 1) * NI)
                pe.wait_ge(w_lo[2], e + 2)
                for a in range(NA):
                    if not first:
                        pe.wait_ge(y3_ready, (e - 1) * NA + a + 1)
                    for c in range(NI):
                        o = c * CAP + a * P
                        left = [hid[:, 1 - r, m, o:o + P] for m in range(2)]
                        right = [piece(s, 2)[:, c * D:(c + 1) * D] for s in SLOT[r]]
                        ins = product(psY[a][:, :], left, right, c, NI)
                    ins.then_inc(y3_ps, 1)

            def step(e, r, known):
                pe.wait_ge(g_lo, (e + 1) * NA)
                for m in range(2):
                    pe.wait_ge(w_lo[m], e + 2)
                for c in range(NI):
                    if known != 0:
                        pe.wait_ge(hid3, (e - 1) * NI + c + 1)
                    for m in range(2):
                        for k in range(KD):
                            o = k * IP + c * P
                            left = [piece(s, m)[:, o:o + P] for s in SLOT[1 - r]]
                            ins = product(psG[c][:, m * CAP:(m + 1) * CAP], left,
                                          [bl[:, 0, k, 0:CAP], bl[:, 1, k, 0:CAP]], k, KD)
                    ins.then_inc(up3_ps, 1)
                if known is None or known + 1 < E2:
                    gathered(e + 1, 1 - r, False)
                if known is None or known > 0:
                    down3(e - 1, r, known == 1)
            gathered(0, 0, True)
            stage3(pe, step)
            down3(E2 - 1, 1 - (E2 - 1) % 2, False)


ORDER = (2, 0, 1)


def S12(small):
    return small[:, 12 * NJ:13 * NJ]


def kernel(**inputs):
    import concourse.bacc as bacc
    from concourse.bass_utils import run_bass_kernel_spmd

    f = {k: np.asarray(v) for k, v in inputs.items()}

    def side(w):
        e = w.shape[0]
        t = np.zeros((e, P, KD, IP), w.dtype)
        t[:, :, :, :I_MLP] = w.reshape(e, I_MLP, KD, P).transpose(0, 3, 2, 1)
        return t

    def down(w):
        e = w.shape[0]
        t = np.zeros((e, IP, D), w.dtype)
        t[:, :I_MLP, :] = w.transpose(0, 2, 1)
        return t.reshape(e, NI, P, D).transpose(0, 2, 1, 3).reshape(e, P, NI * D)

    w1 = side(np.concatenate([f["L0_ffn_Ws1"][None], f["L0_ffn_W1"]]))
    w3 = side(np.concatenate([f["L0_ffn_Ws3"][None], f["L0_ffn_W3"]]))
    w1[0, :, :, I_MLP:I_MLP + E2] = f["L0_ffn_gate_w"].reshape(E2, KD, P).transpose(2, 1, 0)
    arrays = {
        "x": f["x"].reshape(TOK, D),
        "ids": f["itok_BxS_13_99985"].reshape(P, NJ),
        "ctx_t": f["ctx_2048"].reshape(E1, D, KD, P).transpose(0, 3, 2, 1).reshape(E1, P, KD * D),
        "gates": np.broadcast_to(np.concatenate([f["g_xattn"], f["g_ffn"]])[None, :], (P, 2)),
        "w13": np.stack([w1, w3], 2).reshape(E2 + 1, P, 2, KD * IP),
        "w2": down(np.concatenate([f["L0_ffn_Ws2"][None], f["L0_ffn_W2"]])),
        "gate_b": np.broadcast_to(f["L0_ffn_gate_b"][None, :], (P, E2)),
        "const": constants(),
    }
    arrays = {"in_" + k: np.ascontiguousarray(v) for k, v in arrays.items()}
    nc = bacc.Bacc("TRN2", target_bir_lowering=False, num_devices=1)
    args = [nc.dram_tensor(k, v.shape, mybir.dt.from_np(v.dtype), kind="ExternalInput").ap() for k, v in arrays.items()]
    args.append(nc.dram_tensor("out", (TOK + CAP, D), F32, kind="ExternalOutput").ap())
    gated_layer(nc, *args)
    r = run_bass_kernel_spmd(nc, [arrays], core_ids=[0])
    return np.asarray(r.results[0]["out"])[:TOK].reshape(f["x"].shape)
```

```python
import numpy as np
import concourse.bass as bass
from concourse import mybir
from contextlib import ExitStack

F32 = mybir.dt.float32
F32R = mybir.dt.float32r
BF16 = mybir.dt.bfloat16
I32 = mybir.dt.int32
ALU = mybir.AluOpType
ACT = mybir.ActivationFunctionType
AX = mybir.AxisListType

P = 128
TOK, D = 2048, 512
KD = D // P
NJ = TOK // P
E1, VOCAB1 = 4, 25000
NT = NJ + E1 - 1
E2, CAP = 16, 256
I_MLP = 352
NI = 3
IP = NI * P
LOG0 = I_MLP - 2 * P
TB = 4
NB = NJ // TB
BT = TB * P
NA = CAP // P
NQ = E2 * NA
EPS = 1e-5
PAD = TOK

C_ID, C_TRI, C_ONE, C_IOTA = 0, P, 2 * P, 3 * P
C_TOKP, C_TOKJ = 4 * P, 4 * P + NJ
C_KEEP = C_TOKJ + NJ
C_EM = C_KEEP + E2 * NJ
C_SPARE = C_EM + E2
C_END = C_SPARE + NQ


def constants():
    c = np.zeros((P, C_END), np.float32)
    c[:, C_ID:C_ID + P] = np.eye(P)
    c[:, C_TRI:C_TRI + P] = np.triu(np.ones((P, P)), 1)
    c[:, C_ONE:C_ONE + P] = 1.0
    c[:, C_IOTA:C_IOTA + P] = np.arange(P)[None, :]
    c[:, C_TOKP:C_TOKP + NJ] = NJ * np.arange(P)[:, None] - PAD
    c[:, C_TOKJ:C_TOKJ + NJ] = np.arange(NJ)[None, :]
    c[:, C_KEEP:C_KEEP + E2 * NJ] = (np.arange(E2 * NJ) % NJ != 0)[None, :]
    c[:, C_EM:C_EM + E2] = np.arange(E2) - E2
    c[:, C_SPARE:C_SPARE + NQ] = np.arange(P)[:, None] + P * (np.arange(NQ) % NA)[None, :]
    return c



def gated_layer(nc, x, ids, ctx_t, gates, w13, w2, gate_b, const, out):
    stack = ExitStack()
    with stack:
        def sb(name, shape, dt=F32):
            return stack.enter_context(nc.sbuf_tensor(name, shape, dt))

        def sem(name):
            return stack.enter_context(nc.semaphore(name))

        xh = nc.dram_tensor("xh", (TOK, 2 * D), F32).ap()
        xh_rows = xh.rearrange("t (h d) -> (t h) d", h=2)
        xh_tiles = xh.rearrange("(p j) d -> j p d", j=NJ)
        out_tiles = out[0:TOK, :].rearrange("(p j) d -> j p d", j=NJ)

        PC = KD * IP
        assert PC == NI * D
        SW = 3 * PC
        CX = E1 * KD * D
        slot0 = sb("slot0", [P, 2 * SW], F32R)
        arena = sb("arena", [P, 2 * CX + 4 * KD * P], F32R)
        SLOT = [(slot0[:, 0:SW], slot0[:, SW:2 * SW]),
                (arena[:, 0:SW], arena[:, SW:2 * SW])]
        ctx_hi, ctx_lo = arena[:, 0:CX], arena[:, CX:2 * CX]
        hT = [arena[:, 2 * CX + n * KD * P:2 * CX + (n + 1) * KD * P] for n in range(2)]
        gT = [arena[:, 2 * CX + (2 + n) * KD * P:2 * CX + (3 + n) * KD * P] for n in range(2)]
        bl0 = sb("bl0", [P, 2, KD, BT], F32R)
        A_LO = SW + 2 * PC
        A_HID = A_LO + KD * BT
        A_HI = A_HID + 4 * NI * BT
        assert A_HID >= 2 * SW and A_HI + KD * BT <= arena.shape[1]
        hid = arena[:, A_HID:A_HI].rearrange("p (r m n) -> p r m n", r=2, m=2)
        bl = [(bl0[:, 0], bl0[:, 1]),
              tuple(arena[:, o:o + KD * BT].rearrange("p (k n) -> p k n", k=KD) for o in (A_HI, A_LO))]

        raw = sb("raw", [P, 3, PC])
        raw_flat = raw[:, :, :].rearrange("p a b -> p (a b)")
        cst = sb("cst", [P, C_END])
        ident, tri, ones = cst[:, C_ID:C_ID + P], cst[:, C_TRI:C_TRI + P], cst[:, C_ONE:C_ONE + P]
        iota = cst[:, C_IOTA:C_IOTA + P]
        tok_part = [cst[:, c:c + NJ] for c in (C_TOKP, C_TOKJ)]
        gate_in = sb("gate_in", [P, 2])
        tg = sb("tg", [P, 2])
        tok_i = sb("tok_i", [P, NJ], I32)
        bias_b = sb("bias_b", [P, E2])
        small = sb("small", [P, 32 * NJ])
        big = [sb(f"big{n}", [P, NJ, E2]) for n in range(7)]
        qhot = sb("qhot", [P, 2 * NJ * 4 * NQ], BF16)
        small_i = sb("small_i", [P, 6 * NJ], I32)
        cnt_i = sb("cnt_i", [P, 2, E1], I32)
        idx1 = sb("idx1", [P, NT, 2], I32)
        tile_e = sb("tile_e", [P, NT], I32)
        idx2 = sb("idx2", [P, NQ, 2], I32)
        w_slot = sb("w_slot", [P, NQ])
        cur = sb("cur", [P, 8], I32)
        front = sb("front", [P, 4, D])
        xa, h = front[:, 0:2, :], front[:, 2:4, :]
        xb = sb("xb", [P, 2, D])
        s_sb = sb("s_sb", [P, NI * CAP])
        gu = sb("gu", [P, NI * CAP])
        xh_sb = sb("xh_sb", [P, 2, 2 * D])
        stats = sb("stats", [P, 2, 6])
        mv = sb("mv", [P, 2, 2])
        nwt = sb("nwt", [P, 5, 2])
        ht = sb("ht", [P, 4, D])
        ys = sb("ys", [P, 2, D])
        log_sb = sb("log_sb", [P, BT])
        logits = sb("logits", [P, NJ, E2])
        zeros = log_sb
        onehot = [front[:, 2 * k:2 * k + 2, :].rearrange("p a d -> p (a d)").bitcast(BF16)
                  .rearrange("p (b n) -> p b n", n=P) for k in range(2)]
        q_tok = [qhot[:, 0:NJ * 2 * NQ].rearrange("p (b n) -> p b n", b=NJ),
                 log_sb[:, :].bitcast(BF16).rearrange("p (b n) -> p b n", b=NJ)]
        q_w = [qhot[:, (2 + 3 * k) * NJ * NQ:(5 + 3 * k) * NJ * NQ].rearrange("p (b n) -> p b n", b=NJ) for k in range(2)]

        def bank(name):
            return stack.enter_context(nc.psum_tensor(name, [P, 512], F32))
        psT = [bank(f"psT{n}") for n in range(2)]
        psG = [bank(f"psG{n}") for n in range(4)]
        psY = [bank(f"psY{n}") for n in range(2)]

        in_const, in_ids, in_gates, in_bias = (sem(n) for n in ("in_const", "in_ids", "in_gates", "in_bias"))
        raw_here = [sem(f"raw_here{c}") for c in range(3)]
        w_hi = [sem(f"w_hi{c}") for c in range(3)]
        w_lo = [sem(f"w_lo{c}") for c in range(3)]
        ctx_here = [sem(f"ctx_here{n}") for n in range(E1)]
        ctx_hi_done, ctx_lo_done = sem("ctx_hi_done"), sem("ctx_lo_done")
        tg_ready = sem("tg_ready")
        zeroed = sem("zeroed")
        spare_sent = sem("spare_sent")
        chain = sem("chain")
        r1_tot, r1_pre, r1_hot, r1_src, r1_idx = (sem(f"r1_{n}") for n in ("tot", "pre", "hot", "src", "idx"))
        r2_tot, r2_pre, r2_hot, r2_src, r2_idx = (sem(f"r2_{n}") for n in ("tot", "pre", "hot", "src", "idx"))
        r2_whot, r2_wsrc, r2_w = (sem(f"r2_{n}") for n in ("whot", "wsrc", "w"))
        xa_idx, xb_idx, xh_idx = sem("xa_idx"), sem("xb_idx"), sem("xh_idx")
        xa_here = [sem(f"xa_here{n}") for n in range(2)]
        xb_here = [sem(f"xb_here{n}") for n in range(2)]
        xh_sent = [sem(f"xh_sent{n}") for n in range(2)]
        stats_done, mv_done, newton, norm_ready = (sem(n) for n in ("stats_done", "mv_done", "newton", "norm_ready"))
        h_ready, hT_ps, hT_hi, hT_lo = (sem(n) for n in ("h_ready", "hT_ps", "hT_hi", "hT_lo"))
        p_ps, s_ready, gu_ready = (sem(n) for n in ("p_ps", "s_ready", "gu_ready"))
        gT_ps, gT_hi, gT_lo = (sem(n) for n in ("gT_ps", "gT_hi", "gT_lo"))
        y_ps, x1_ready, xh_ready = sem("y_ps"), sem("x1_ready"), sem("xh_ready")
        ht_here = [sem(f"ht_here{n}") for n in range(4)]
        x1_here = [sem(f"x1_here{n}") for n in range(2)]
        bT_ps, bT_hi, bT_lo = sem("bT_ps"), sem("bT_hi"), sem("bT_lo")
        up_ps, silu_ready, hid_ready, hid_hi, hid_lo = (
            sem(n) for n in ("up_ps", "silu_ready", "hid_ready", "hid_hi", "hid_lo"))
        log_copied, log_ps, log_ready = sem("log_copied"), sem("log_ps"), sem("log_ready")
        y2_ps, y2_copied, o_ready = sem("y2_ps"), sem("y2_copied"), sem("o_ready")
        out_sent = [sem(f"out_sent{n}") for n in range(2)]
        soft_in, soft = sem("soft_in"), sem("soft")
        g_idx, add_idx = sem("g_idx"), sem("add_idx")
        g_here = [sem(f"g_here{n}") for n in range(4)]
        g_ps, g_hi, g_lo = sem("g_ps"), sem("g_hi"), sem("g_lo")
        up3_ps, silu3, hid3, hid3_hi, hid3_lo = (sem(n) for n in ("up3_ps", "silu3", "hid3", "hid3_hi", "hid3_lo"))
        y3_ps, y3_ready = sem("y3_ps"), sem("y3_ready")
        added = [sem(f"added{n}") for n in range(2)]

        EARLY = NJ - 2

        block = stack.enter_context(nc.Block())

        def as_f32(ap):
            return ap.bitcast(F32)

        def landed(q, par):
            return 8 * q + 8 * (2 - par)

        def chunks(ap):
            return ap.rearrange("p (k t) -> p k t", k=KD)

        FIRST, LOOP0, LOOP1, LAST = -2, 5, 17, NT + 2

        def stage1(eng, step):
            for t in range(FIRST, LOOP0):
                step(t, t % 2, t)
            with eng.Fori(0, (LOOP1 - LOOP0) // 2) as i:
                step(eng.snap(i * 2 + LOOP0), LOOP0 % 2, None)
                step(eng.snap(i * 2 + (LOOP0 + 1)), (LOOP0 + 1) % 2, None)
            for t in range(LOOP1, LAST):
                step(t, t % 2, t)

        def have(known, k):
            return known is None or 0 <= known + k < NT

        def had(known, k):
            return known is None or (known > FIRST and 0 <= known - 1 + k < NT)

        def stage3(eng, step):
            for e in range(3):
                step(e, e % 2, e)
            with eng.Fori(0, E2 // 2 - 3) as i:
                step(eng.snap(i * 2 + 3), 1, None)
                step(eng.snap(i * 2 + 4), 0, None)
            for e in range(E2 - 3, E2):
                step(e, e % 2, e)

        def ctx_raw(e):
            if e < 2:
                return raw_flat[:, e * KD * D:(e + 1) * KD * D]
            return (ht if e == 2 else xh_sb)[:, :, :].rearrange("p a d -> p (a d)")

        def piece(ap, c):
            return ap[:, c * PC:(c + 1) * PC]

        @block.sync
        def _(sp):
            def load(s, c, known=True):
                if not (known and isinstance(s, int) and s == 0):
                    sp.wait_ge(w_lo[c], s)
                src = (w13[bass.ds(s, 1), :, c, :] if c < 2 else w2[bass.ds(s, 1), :, :])
                sp.dma_start(raw[:, c, :], src.rearrange("a p n -> (a p) n")).then_inc(raw_here[c], 16)

            sp.dma_start(tok_i[:, :], ids).then_inc(in_ids, 16)
            sp.dma_start(cst[:, :], const).then_inc(in_const, 16)
            sp.dma_start(gate_in[:, :], gates).then_inc(in_gates, 16)
            sp.dma_start(bias_b[:, :], gate_b).then_inc(in_bias, 16)
            for e in range(E1):
                sp.dma_start(ctx_raw(e), ctx_t[e, :, :]).then_inc(ctx_here[e], 16)
            sp.wait_ge(zeroed, 1)
            for a in range(NA):
                sp.dma_start(out[TOK + a * P:TOK + (a + 1) * P, :], zeros[:, :]).then_inc(spare_sent, 16)
            sp.wait_ge(ctx_lo_done, E1)
            for c in range(3):
                load(0, c)
            for n in range(2):
                last = NT - 1 - (NT - 1 - n) % 2
                sp.wait_ge(xh_sent[n], landed(last, n))

            def load_ht(j):
                if j >= 4:
                    sp.wait_ge(bT_ps, j - 3)
                sp.dma_start(ht[:, j % 4, :], xh_tiles[j, :, D:2 * D]).then_inc(ht_here[j % 4], 16)

            for j in range(4):
                load_ht(j)
            for c in range(3):
                load(1, c)
            for j in range(4, NJ):
                load_ht(j)
            for c in range(2):
                load(2, c)

            def store(j):
                sp.wait_ge(o_ready, j + 1)
                sp.dma_start(out_tiles[j, :, :], xh_sb[:, j % 2, 0:D]).then_inc(out_sent[j % 2], 16)

            for j in range(NJ):
                if j >= 2:
                    sp.wait_ge(o_ready, j - 1)
                sp.dma_start(xb[:, j % 2, :], xh_tiles[j, :, 0:D]).then_inc(x1_here[j % 2], 16)
                if j >= 1:
                    store(j - 1)
            store(NJ - 1)
            load(3, 0)
            with sp.Fori(2, E2 - 1) as s:
                load(sp.snap(s + 1), 1)
                load(s, 2)
                load(sp.snap(s + 2), 0)
            load(E2, 1)
            load(E2 - 1, 2)
            load(E2, 2)
            for a in range(NA):
                sp.wait_ge(added[a], 16 * E2)

        @block.gpsimd
        def _(pool):
            pool.memset(zeros[:, :], 0.0).then_inc(zeroed, 1)

            def index(n, table, q, col, done, count):
                pool.tensor_copy(cur[:, n:n + 1], table[:, bass.ds(q, 1), col]).then_inc(done, 1)
                pool.wait_ge(done, count)
                pool.nop(nofuse=True)
                return bass.IndirectOffsetOnAxis(ap=cur[:, n:n + 1], axis=0)

            pool.wait_ge(r1_idx, 1)
            for q in range(2):
                pool.indirect_dma_start(xa[:, q, :], None, x, index(q, idx1, q, 0, xa_idx, q + 1)).then_inc(xa_here[q], 16)

            def low_ctx(e, part=0, parts=1):
                pool.wait_ge(ctx_hi_done, e + 1)
                pool.wait_ge(ctx_lo_done, e)
                n = KD * D // parts
                here = slice(part * n, (part + 1) * n)
                c = slice(e * KD * D + part * n, e * KD * D + (part + 1) * n)
                i = pool.tensor_tensor(ctx_lo[:, c], ctx_raw(e)[:, here], as_f32(ctx_hi[:, c]), ALU.subtract)
                if part == parts - 1:
                    i.then_inc(ctx_lo_done, 1)

            low_ctx(E1 - 2)

            def step(t, par, known):
                if have(known, 0):
                    if had(known, -1):
                        pool.wait_ge(x1_ready, t - 1)
                    i = index(2 + par, idx1, t, 0, xb_idx, t + 1)
                    pool.indirect_dma_start(xb[:, par, :], None, x, i).then_inc(xb_here[par], 16)
                if have(known, 4):
                    pool.wait_ge(h_ready, t + 3)
                    i = index(par, idx1, t + 4, 0, xa_idx, t + 5)
                    pool.indirect_dma_start(xa[:, par, :], None, x, i).then_inc(xa_here[par], 16)
                if have(known, -2):
                    pool.wait_ge(xh_ready, t - 1)
                    i = index(4 + par, idx1, t - 2, 1, xh_idx, t - 1)
                    pool.indirect_dma_start(xh, i, xh_sb[:, par, :], None,
                                            bounds_check=TOK - 1, oob_is_err=False).then_inc(xh_sent[par], 16)

            for t in range(FIRST, LOOP0):
                step(t, t % 2, t)
                if t in (FIRST, FIRST + 1):
                    low_ctx(E1 - 1, t - FIRST, 2)
            with pool.Fori(0, (LOOP1 - LOOP0) // 2 - 1) as i:
                step(pool.snap(i * 2 + LOOP0), LOOP0 % 2, None)
                step(pool.snap(i * 2 + (LOOP0 + 1)), (LOOP0 + 1) % 2, None)
            for t in range(LOOP1 - 2, LAST):
                step(t, t % 2, t)

            def base(j):
                r = j % 2
                pool.wait_ge(x1_here[r], landed(j, r))
                pool.wait_ge(y2_copied, j + 1)
                if j >= 2:
                    pool.wait_ge(out_sent[r], landed(j - 2, r))
                pool.tensor_tensor(xh_sb[:, r, 0:D], ys[:, r, :], xb[:, r, :], ALU.add).then_inc(o_ready, 1)

            for j in range(EARLY):
                base(j)

            def gather(e, r, free):
                for a in range(NA):
                    n = 2 * r + a
                    if free:
                        pool.wait_ge(g_ps, (e - 2) * NA + a + 1)
                    i = index(n, idx2, e * NA + a, 0, g_idx, e * NA + a + 1)
                    pool.indirect_dma_start(ht[:, n, :], None, xh_rows, i).then_inc(g_here[n], 16)

            def add(e, first):
                for a in range(NA):
                    pool.wait_ge(y3_ready, e * NA + a + 1)
                    if not first and a == 0:
                        for b in range(NA):
                            pool.wait_ge(added[b], e * 16)
                    i = index(4 + a, idx2, e * NA + a, 1, add_idx, e * NA + a + 1)
                    pool.indirect_dma_start(out, i, ys[:, a, :], None,
                                            compute_op=ALU.add).then_inc(added[a], 16)

            pool.wait_ge(r2_idx, 1)
            gather(0, 0, False)
            for j in range(EARLY, NJ):
                base(j)
            gather(1, 1, False)
            pool.wait_ge(spare_sent, 16 * NA)
            for r in range(2):
                pool.wait_ge(out_sent[r], landed(NJ - 2 + r, r))
            gather(2, 0, True)
            gather(3, 1, True)
            gather(4, 0, True)
            add(0, True)
            with pool.Fori(0, E2 // 2 - 3) as i:
                gather(pool.snap(i * 2 + 5), 1, True)
                add(pool.snap(i * 2 + 1), False)
                gather(pool.snap(i * 2 + 6), 0, True)
                add(pool.snap(i * 2 + 2), False)
            gather(E2 - 1, 1, True)
            for e in range(E2 - 5, E2):
                add(e, False)

        @block.scalar
        def _(act):
            act.wait_ge(in_gates, 16)
            act.activation(tg[:, :], gate_in[:, :], ACT.Tanh).then_inc(tg_ready, 1)
            act.activation(s_sb[:, D:D + 2], gate_in[:, :], ACT.Silu)
            for e in range(E1):
                act.wait_ge(ctx_here[e], 16)
                act.activation(ctx_hi[:, e * KD * D:(e + 1) * KD * D], ctx_raw(e), ACT.Copy).then_inc(ctx_hi_done, 1)

            def norm(dst, src, col, done):
                act.activation(dst, src, ACT.Identity, scale=nwt[:, 3, col:col + 1],
                               bias=nwt[:, 4, col:col + 1]).then_inc(done, 1)

            def step(t, par, known):
                if have(known, -1):
                    act.wait_ge(gT_ps, t)
                    act.activation(gT[0], psT[1][:, :], ACT.Copy).then_inc(gT_hi, 1)
                if have(known, 0):
                    act.wait_ge(p_ps, t + 1)
                    if had(known, 0):
                        act.wait_ge(gu_ready, t)
                    act.activation(s_sb[:, 0:D], psG[0][:, :], ACT.Silu).then_inc(s_ready, 1)
                if have(known, 1):
                    act.wait_ge(hT_ps, t + 2)
                    act.activation(hT[0], psT[0][:, :], ACT.Copy).then_inc(hT_hi, 1)
                act.wait_ge(norm_ready, t + 3)
                if have(known, 2):
                    if had(known, 1):
                        act.wait_ge(hT_ps, t + 1)
                    norm(h[:, par, :], xa[:, par, :], 0, h_ready)
                if have(known, -2):
                    norm(xh_sb[:, par, D:2 * D], xh_sb[:, par, 0:D], 1, xh_ready)
            stage1(act, step)

            def split(s, c, r):
                act.wait_ge(raw_here[c], 16 * s + 16)
                act.activation(piece(SLOT[r][0], c), raw[:, c, :], ACT.Copy).then_inc(w_hi[c], 1)

            for c in range(3):
                split(0, c, 0)

            def transposed(j):
                act.wait_ge(bT_ps, j + 1)
                b = j // TB
                if b >= 2:
                    act.wait_ge(up_ps, seq_end(b - 2))
                act.activation(bl[b % 2][0][:, :, (j % TB) * P:(j % TB + 1) * P], chunks(psT[j % 2][:, :]),
                               ACT.Copy).then_inc(bT_hi, 1)

            def silu(n):
                b, c = SEQ[n]
                act.wait_ge(up_ps, n + 1)
                if n:
                    act.wait_ge(hid_ready, n)
                act.activation(s_sb[:, 0:BT], psG[2 * (n % 2)][:, :], ACT.Silu).then_inc(silu_ready, 1)
                if c == 2:
                    if b:
                        act.wait_ge(log_ps, b)
                    else:
                        act.wait_ge(spare_sent, 16 * NA)
                    act.activation(log_sb[:, :], psG[2 * (n % 2)][:, :], ACT.Copy).then_inc(log_copied, 1)

            def high(n):
                b, c = SEQ[n]
                act.wait_ge(hid_ready, n + 1)
                if b >= 2:
                    act.wait_ge(y2_ps, TB * (b - 1))
                act.activation(hid[:, b % 2, 0, c * BT:(c + 1) * BT], gu[:, 0:BT], ACT.Copy).then_inc(hid_hi, 1)

            def hidden(n):
                silu(n)
                high(n)

            def rows(j):
                act.wait_ge(y2_ps, j + 1)
                if j >= 2:
                    act.wait_ge(o_ready, j - 1)
                act.activation(ys[:, j % 2, :], psY[j % 2][:, :], ACT.Copy, scale=tg[:, 1:2]).then_inc(y2_copied, 1)

            def router(n, dst, src, f, **kw):
                act.wait_ge(soft_in, n)
                act.activation(dst[:, :, :], src[:, :, :], f, **kw).then_inc(soft, 1)

            for j in range(TB):
                transposed(j)
            for b in range(2):
                for i in range(NI):
                    hidden(NI * b + i)
                    if i < 2:
                        for j in (TB * (b + 1) + 2 * i, TB * (b + 1) + 2 * i + 1):
                            transposed(j)
                if b == 0:
                    split(1, 0, 1)
                    split(1, 1, 1)
            for j in range(TB * (NB - 1), NJ):
                rows(j - 3 * TB)
                transposed(j)
            for j in range(TB, 2 * TB):
                rows(j)
            hidden(2 * NI)
            hidden(2 * NI + 1)
            router(1, big[1], big[0], ACT.Exp, scale=-1.0)
            router(2, big[3], big[2], ACT.Ln)
            router(3, big[5], big[3], ACT.Sqrt)
            for n in range(2 * NI + 2, NB * NI - 1):
                hidden(n)
            silu(NB * NI - 1)
            for j in range(TB * (NB - 2), NJ):
                if j == TB * (NB - 2) + 2:
                    high(NB * NI - 1)
                rows(j)

            def gathered(e):
                for a in range(NA):
                    act.wait_ge(g_ps, e * NA + a + 1)
                    act.activation(bl[0][0][:, :, a * P:(a + 1) * P], chunks(psT[a][:, :]), ACT.Copy).then_inc(g_hi, 1)

            def rows3(e, first):
                if first:
                    act.wait_ge(r2_w, 1)
                for a in range(NA):
                    act.wait_ge(y3_ps, e * NA + a + 1)
                    if not first:
                        act.wait_ge(added[a], e * 16)
                    act.activation(ys[:, a, :], psY[a][:, :], ACT.Copy,
                                   scale=w_slot[:, bass.ds(e * NA + a, 1)]).then_inc(y3_ready, 1)

            def step(e, r, known):
                more = known is None or known + 1 < E2

                def silu(c):
                    act.wait_ge(up3_ps, e * NI + c + 1)
                    if known != 0 and c == 0:
                        act.wait_ge(hid3, e * NI)
                    act.activation(s_sb[:, c * CAP:(c + 1) * CAP], psG[c][:, 0:CAP], ACT.Silu).then_inc(silu3, 1)

                def high(c):
                    act.wait_ge(hid3, e * NI + c + 1)
                    if known != 0 and c == 0:
                        act.wait_ge(y3_ps, e * NA - NA)
                    act.activation(hid[:, r, 0, c * CAP:(c + 1) * CAP], gu[:, c * CAP:(c + 1) * CAP],
                                   ACT.Copy).then_inc(hid3_hi, 1)
                if more:
                    split(e + 2, 1, r)
                silu(0)
                if known != 0:
                    act.wait_ge(y3_ps, e * NA - NA)
                split(e + 1, 2, 1 - r)
                high(0)
                silu(1)
                high(1)
                silu(2)
                if more:
                    gathered(e + 1)
                high(2)
                if known is None or known + 3 <= E2:
                    split(e + 3, 0, 1 - r)
                if known is None or known > 0:
                    rows3(e - 1, known == 1)
            gathered(0)
            split(2, 0, 0)
            stage3(act, step)
            rows3(E2 - 1, False)

        @block.vector
        def _(dve):
            links = [0]

            def link(ins):
                links[0] += 1
                ins.then_inc(chain, 1)
                dve.wait_ge(chain, links[0])

            def S(n, w=1):
                return small[:, n * NJ:(n + w) * NJ]

            def SI(n, w=1):
                return small_i[:, n * NJ:(n + w) * NJ]

            def over(ap, n):
                return ap.unsqueeze(2).to_broadcast([P, ap.shape[1], n])

            def along(ap, n):
                return ap.unsqueeze(1).to_broadcast([P, n, ap.shape[1]])

            def low_ctx(e):
                dve.wait_ge(ctx_hi_done, e + 1)
                c = slice(e * KD * D, (e + 1) * KD * D)
                dve.tensor_tensor(ctx_lo[:, c], ctx_raw(e), as_f32(ctx_hi[:, c]), ALU.subtract).then_inc(ctx_lo_done, 1)

            dve.wait_ge(in_ids, 16)
            link(dve.tensor_copy(S(0), tok_i[:, :]))
            for e in range(1, E1):
                link(dve.tensor_scalar(S(e), S(0), float(VOCAB1 // E1 * e), None, ALU.is_ge))
            link(dve.tensor_scalar(S(4), S(1), -1.0, 1.0, ALU.mult, ALU.add))
            link(dve.tensor_tensor(S(5, 2), S(1, 2), S(2, 2), ALU.subtract))
            link(dve.tensor_copy(S(7), S(3)))
            dve.wait_ge(in_const, 16)
            link(dve.tensor_tensor_scan(S(8, E1), cst[:, C_KEEP:C_KEEP + E1 * NJ], S(4, E1), 0.0, ALU.mult, ALU.add))
            run = S(8, E1).rearrange("p (e j) -> p e j", e=E1)
            dve.tensor_copy(S(12)[:, 0:E1], run[:, :, NJ - 1]).then_inc(r1_tot, 1)
            dve.wait_ge(r1_pre, 1)
            link(dve.tensor_scalar(cnt_i[:, 0, :], psY[0][:, E1:2 * E1], float(P - 1), None, ALU.add))
            link(dve.tensor_scalar(cnt_i[:, 1, :], cnt_i[:, 0, :], -P, None, ALU.bitwise_and))
            link(dve.tensor_copy(S(13)[:, 0:E1], cnt_i[:, 1, :]))
            link(dve.tensor_tensor_scan(S(14)[:, 0:E1], ones[:, 0:E1], S(13)[:, 0:E1], 0.0, ALU.mult, ALU.add))
            link(dve.tensor_tensor(S(15)[:, 0:E1], S(14)[:, 0:E1], S(13)[:, 0:E1], ALU.subtract))
            link(dve.tensor_tensor(S(16)[:, 0:E1], S(15)[:, 0:E1], psY[0][:, 0:E1], ALU.add))
            link(dve.tensor_tensor(S(17, E1).rearrange("p (e j) -> p e j", e=E1), run, over(S(16)[:, 0:E1], NJ), ALU.add))
            link(dve.tensor_tensor(S(21, E1), S(17, E1), S(4, E1), ALU.mult))
            link(dve.tensor_reduce(S(25), S(21, E1).rearrange("p (e j) -> p j e", e=E1), AX.X, ALU.add))
            link(dve.tensor_scalar(SI(0), S(25), -1.0, None, ALU.add))
            link(dve.tensor_scalar(SI(1), SI(0), P - 1, None, ALU.bitwise_and))
            link(dve.tensor_scalar(SI(2), SI(0), 7, None, ALU.arith_shift_right))
            link(dve.tensor_copy(S(26, 2), SI(1, 2)))
            dve.tensor_tensor(onehot[0], along(iota, NJ), over(S(26), P), ALU.is_equal)
            q = q_tok[0]
            link(dve.tensor_tensor(q_w[0][:, :, 0:NT], along(iota[:, 0:NT], NJ), over(S(27), NT), ALU.is_equal))
            dve.tensor_tensor(q[:, :, 0:NT], q_w[0][:, :, 0:NT], over(tok_part[0], NT), ALU.mult)
            dve.tensor_tensor(q[:, :, NT:2 * NT], q_w[0][:, :, 0:NT], over(tok_part[1], NT), ALU.mult).then_inc(r1_hot, 1)
            link(dve.tensor_scalar(S(28, 2)[:, 0:NT], iota[:, 0:NT], float(P), S(14)[:, 0:1], ALU.mult, ALU.is_ge))
            for e in range(1, E1 - 1):
                link(dve.tensor_scalar(S(30, 2)[:, 0:NT], iota[:, 0:NT], float(P), S(14)[:, e:e + 1], ALU.mult, ALU.is_ge))
                link(dve.tensor_tensor(S(28, 2)[:, 0:NT], S(28, 2)[:, 0:NT], S(30, 2)[:, 0:NT], ALU.add))
            link(dve.tensor_copy(tile_e[:, :], S(28, 2)[:, 0:NT]))
            low_ctx(0)
            dve.wait_ge(r1_src, 1)
            link(dve.tensor_copy(S(30, 2)[:, 0:NT], psY[1][:, 0:NT]))
            src = S(28, 2)[:, 0:NT]
            link(dve.scalar_tensor_tensor(src, psY[1][:, NT:2 * NT], float(PAD), S(30, 2)[:, 0:NT], ALU.add, ALU.add))
            dve.tensor_scalar(idx1[:, :, 0], src, float(TOK - 1), None, ALU.min)
            dve.tensor_copy(idx1[:, :, 1], src).then_inc(r1_idx, 1)

            low_ctx(1)
            dve.wait_ge(tg_ready, 1)

            NEWTON = 11

            def step(t, par, known):
                one, two = have(known, 2), have(known, -2)
                if two:
                    dve.wait_ge(y_ps, t - 1)
                    dve.wait_ge(xb_here[par], landed(t - 2, par))
                    if known == 2:
                        dve.wait_ge(ctx_lo_done, E1)
                    if known is None or known >= 4:
                        dve.wait_ge(xh_sent[par], landed(t - 4, par))
                    dve.scalar_tensor_tensor(xh_sb[:, par, 0:D], psY[0][:, :], tg[:, 0:1], xb[:, par, :],
                                             ALU.mult, ALU.add).then_inc(x1_ready, 1)
                def low_h():
                    dve.wait_ge(hT_hi, t + 2)
                    dve.tensor_tensor(hT[1], psT[0][:, :], as_f32(hT[0]), ALU.subtract).then_inc(hT_lo, 1)

                def gate():
                    dve.wait_ge(s_ready, t + 1)
                    if had(known, 0):
                        dve.wait_ge(gT_ps, t)
                    dve.tensor_tensor(gu[:, 0:D], s_sb[:, 0:D], psG[0][:, :], ALU.mult).then_inc(gu_ready, 1)

                if known == FIRST + 1:
                    low_h()
                if known == 0:
                    gate()
                    low_h()

                def low_g():
                    if have(known, -1):
                        dve.wait_ge(gT_hi, t)
                        dve.tensor_tensor(gT[1], psT[1][:, :], as_f32(gT[0]), ALU.subtract).then_inc(gT_lo, 1)
                cs = slice(0 if one else 1, 2 if two else 1)
                i = None
                if one:
                    dve.wait_ge(xa_here[par], landed(t + 2, par))
                    i = dve.bn_stats(stats[:, 0, :], xa[:, par, :])
                if two:
                    dve.wait_ge(x1_ready, t - 1)
                    i = dve.bn_stats(stats[:, 1, :], xh_sb[:, par, 0:D])
                k = t + 2
                if not (one or two):
                    dve.tensor_copy(stats[:, 0, 0:1], cst[:, 0:1]).then_inc(norm_ready, 1)
                else:
                    i.then_inc(stats_done, 1)
                low_g()
                if one or two:
                    dve.wait_ge(stats_done, NORMS(k, known))
                    dve.nop(nofuse=True)
                    if one:
                        i = dve.bn_aggr(mv[:, 0, :], stats[:, 0, :])
                    if two:
                        i = dve.bn_aggr(mv[:, 1, :], stats[:, 1, :])
                    i.then_inc(mv_done, 1)
                    dve.wait_ge(mv_done, NORMS(k, known))
                    base = (NORMS(k, known) - 1) * NEWTON
                    n = [0]

                    def nw(ins):
                        n[0] += 1
                        ins.then_inc(newton, 1)
                        dve.wait_ge(newton, base + n[0])
                    V, Y, T, R, B = (nwt[:, m, cs] for m in range(5))
                    nw(dve.tensor_scalar(V, mv[:, cs, 1], EPS, 0.5, ALU.add, ALU.mult))
                    nw(dve.tensor_scalar(Y.bitcast(I32), V.bitcast(I32), -0.5, float(0x5f3759df - (1 << 22) - (1 << 31)),
                                         ALU.mult, ALU.add))
                    for m in range(3):
                        nw(dve.tensor_tensor(T, V, Y, ALU.mult))
                        nw(dve.tensor_tensor(T, T, Y, ALU.mult))
                        if m == 2:
                            if had(known, 2):
                                dve.wait_ge(h_ready, t + 2)
                            if had(known, -2):
                                dve.wait_ge(xh_ready, t - 2)
                        nw(dve.scalar_tensor_tensor(R if m == 2 else Y, T, -1.5, Y, ALU.add, ALU.mult))
                    assert n[0] == NEWTON
                    dve.scalar_tensor_tensor(B, mv[:, cs, 0], -1.0, R, ALU.mult, ALU.mult).then_inc(norm_ready, 1)
                if have(known, 0) and known != 0:
                    gate()
                if have(known, 1) and known not in (FIRST + 1, 0):
                    low_h()

            def NORMS(k, known):
                return k + 1
            stage1(dve, step)

            def split(s, c, r):
                dve.wait_ge(w_hi[c], s + 1)
                dve.tensor_tensor(piece(SLOT[r][1], c), raw[:, c, :], as_f32(piece(SLOT[r][0], c)),
                                  ALU.subtract).then_inc(w_lo[c], 1)

            for c in range(3):
                split(0, c, 0)

            def transposed(j):
                dve.wait_ge(bT_hi, j + 1)
                b = bl[(j // TB) % 2]
                s = slice((j % TB) * P, (j % TB + 1) * P)
                dve.tensor_tensor(b[1][:, :, s], chunks(psT[j % 2][:, :]), as_f32(b[0][:, :, s]),
                                  ALU.subtract).then_inc(bT_lo, 1)

            def gate(n):
                dve.wait_ge(silu_ready, n + 1)
                if n:
                    dve.wait_ge(hid_hi, n)
                    dve.wait_ge(hid_lo, n)
                dve.tensor_tensor(gu[:, 0:BT], s_sb[:, 0:BT], psG[2 * (n % 2) + 1][:, :], ALU.mult).then_inc(hid_ready, 1)

            def low(n):
                b, c = SEQ[n]
                dve.wait_ge(hid_hi, n + 1)
                s = slice(c * BT, (c + 1) * BT)
                dve.tensor_tensor(hid[:, b % 2, 1, s], gu[:, 0:BT], as_f32(hid[:, b % 2, 0, s]),
                                  ALU.subtract).then_inc(hid_lo, 1)

            def hidden(n):
                gate(n)
                low(n)

            def take_logits(b):
                dve.wait_ge(log_ps, b + 1)
                src = psY[1][:, :].rearrange("p (j n) -> p j n", j=TB)[:, :, LOG0:LOG0 + E2]
                dve.tensor_copy(logits[:, b * TB:(b + 1) * TB, :], src).then_inc(log_ready, 1)

            for j in range(TB):
                transposed(j)
            for b in range(2):
                for i in range(NI):
                    hidden(NI * b + i)
                    if i == 1:
                        take_logits(b)
                    if i < 2:
                        for j in (TB * (b + 1) + 2 * i, TB * (b + 1) + 2 * i + 1):
                            transposed(j)
                if b == 0:
                    split(1, 0, 1)
                    split(1, 1, 1)
            for j in range(TB * (NB - 1), NJ):
                transposed(j)
            hidden(2 * NI)
            hidden(2 * NI + 1)
            take_logits(NB - 2)
            take_logits(NB - 1)

            B = [x_[:, :, :] for x_ in big]
            L = logits[:, :, :]
            dve.wait_ge(log_ready, NB)
            dve.scalar_tensor_tensor(B[0], L, -1.0, L, ALU.mult, ALU.max).then_inc(soft_in, 1)
            dve.wait_ge(soft, 1)
            dve.tensor_scalar(B[2], B[1], 1.0, None, ALU.add).then_inc(soft_in, 1)
            dve.wait_ge(soft_in, 2)
            link(dve.tensor_scalar(B[4], B[2], -1.0, None, ALU.add))
            link(dve.tensor_scalar(B[0], B[4], 1e-30, None, ALU.max))
            link(dve.reciprocal(B[0], B[0]))
            link(dve.tensor_tensor(B[0], B[0], B[1], ALU.mult))
            link(dve.scalar_tensor_tensor(B[4], B[4], 0.0, B[1], ALU.is_equal, ALU.mult))
            link(dve.scalar_tensor_tensor(B[4], L, 0.0, B[4], ALU.max, ALU.add))
            dve.wait_ge(soft, 2)
            link(dve.tensor_tensor(B[6], B[3], B[0], ALU.mult))
            dve.tensor_tensor(B[3], B[6], B[4], ALU.add).then_inc(soft_in, 1)
            dve.wait_ge(soft, 3)
            hidden(2 * NI + 2)
            dve.wait_ge(in_bias, 16)
            link(dve.tensor_tensor(B[0], B[5], along(bias_b[:, :], NJ), ALU.add))
            em = along(cst[:, C_EM:C_EM + E2], NJ)
            pick = [B[1], B[2]]
            for k in range(2):
                m, i = S(k), S(2 + k)
                link(dve.tensor_reduce(m, B[0], AX.X, ALU.max))
                link(dve.tensor_tensor(B[3], B[0], over(m, E2), ALU.is_equal))
                link(dve.tensor_tensor(B[3], B[3], em, ALU.mult))
                link(dve.tensor_reduce(i, B[3], AX.X, ALU.min))
                link(dve.tensor_tensor(pick[k], em, over(i, E2), ALU.is_equal))
                if k == 0:
                    hidden(2 * NI + 3)
                    link(dve.scalar_tensor_tensor(B[0], pick[0], -3e38, B[0], ALU.mult, ALU.add))
            by_e = B[3].rearrange("p j e -> p (j e)").rearrange("p (e j) -> p j e", e=E2)
            link(dve.tensor_tensor(by_e, pick[0], pick[1], ALU.add))
            flat = [b_.rearrange("p j e -> p (j e)") for b_ in B]
            link(dve.tensor_tensor_scan(flat[4], cst[:, C_KEEP:C_KEEP + E2 * NJ], flat[3], 0.0, ALU.mult, ALU.add))
            count = flat[4].rearrange("p (e j) -> p e j", e=E2)
            dve.tensor_copy(S(4), count[:, :, NJ - 1]).then_inc(r2_tot, 1)
            hidden(2 * NI + 4)
            gate(NB * NI - 1)
            dve.wait_ge(r2_pre, 1)
            link(dve.tensor_tensor(flat[0].rearrange("p (e j) -> p e j", e=E2), count, over(psT[0][:, 0:E2], NJ), ALU.add))
            pos = flat[0].rearrange("p (e j) -> p j e", e=E2)
            for k in range(2):
                link(dve.tensor_tensor(B[6], pick[k], pos, ALU.mult))
                link(dve.tensor_reduce(S(8 + k), B[6], AX.X, ALU.add))
            low(NB * NI - 1)
            link(dve.scalar_tensor_tensor(S(10, 2), S(2, 2), float(CAP), S(8, 2), ALU.mult, ALU.add))
            link(dve.tensor_scalar(SI(0, 2), S(10, 2), float(E2 * CAP - 1), None, ALU.add))
            link(dve.tensor_scalar(SI(2, 2), SI(0, 2), P - 1, None, ALU.bitwise_and))
            link(dve.tensor_scalar(SI(4, 2), SI(0, 2), 7, None, ALU.arith_shift_right))
            link(dve.tensor_copy(S(12, 4), SI(2, 4)))
            link(dve.tensor_scalar(S(16, 2), S(8, 2), float(CAP), 1024.0, ALU.is_gt, ALU.mult))
            link(dve.tensor_tensor(S(14, 2), S(14, 2), S(16, 2), ALU.add))
            qn = [along(iota[:, 0:NQ], NJ), [over(S(14 + k), NQ) for k in range(2)]]
            for k in range(2):
                dve.tensor_tensor(onehot[k], along(iota, NJ), over(S(12 + k), P), ALU.is_equal)
                q, tile = q_tok[k], q_w[k][:, :, 0:NQ]
                link(dve.tensor_tensor(tile, qn[0], qn[1][k], ALU.is_equal))
                for m in range(2):
                    i = dve.tensor_tensor(q[:, :, m * NQ:(m + 1) * NQ], tile, over(tok_part[m], NQ), ALU.mult)
                i.then_inc(r2_hot, 1)
            dve.wait_ge(r2_src, 1)
            U = [S(n, 2) for n in (16, 18, 20, 22)]
            link(dve.tensor_copy(U[3], psT[1][:, 0:NQ]))
            link(dve.tensor_tensor(U[3], psT[1][:, NQ:2 * NQ], U[3], ALU.add))
            link(dve.tensor_scalar(U[0], U[3], 0.0, None, ALU.is_equal))
            link(dve.tensor_scalar(U[1], U[3], 2.0, 2.0 * PAD + 1, ALU.mult, ALU.add))
            link(dve.scalar_tensor_tensor(idx2[:, :, 0], U[0], -2.0 * PAD, U[1], ALU.mult, ALU.add))
            link(dve.tensor_tensor(U[2], U[0], cst[:, C_SPARE:C_SPARE + NQ], ALU.mult))
            dve.scalar_tensor_tensor(idx2[:, :, 1], U[3], float(PAD), U[2], ALU.add, ALU.add).then_inc(r2_idx, 1)
            for k in range(2):
                link(dve.tensor_tensor(B[6], pick[k], B[5], ALU.mult))
                link(dve.tensor_reduce(S(5 + k), B[6], AX.X, ALU.add))
            link(dve.tensor_tensor(S(7), S(5), S(6), ALU.add))
            link(dve.reciprocal(S(7), S(7)))
            for k in range(2):
                link(dve.scalar_tensor_tensor(S(5 + k), S(5 + k), tg[:, 1:2], S(7), ALU.mult, ALU.mult))
            dve.wait_ge(r2_idx, 1)
            short = S(22, 2)[:, 0:NJ].bitcast(BF16)
            rest = S(5, 2)
            for m in range(3):
                link(dve.tensor_copy(short, rest))
                link(dve.tensor_copy(S(24 + 2 * m, 2), short))
                if m < 2:
                    link(dve.tensor_tensor(S(30, 2), rest, S(24 + 2 * m, 2), ALU.subtract))
                    rest = S(30, 2)
            def weigh(k):
                for m in (2, 1, 0):
                    w = over(S(24 + 2 * m, 2)[:, k * NJ:(k + 1) * NJ], NQ)
                    i = dve.tensor_tensor(q_w[k][:, :, m * NQ:(m + 1) * NQ], q_w[k][:, :, 0:NQ], w, ALU.mult)
                i.then_inc(r2_whot, 1)
            def gathered(e):
                for a in range(NA):
                    dve.wait_ge(g_hi, e * NA + a + 1)
                    s = slice(a * P, (a + 1) * P)
                    dve.tensor_tensor(bl[0][1][:, :, s], chunks(psT[a][:, :]), as_f32(bl[0][0][:, :, s]),
                                      ALU.subtract).then_inc(g_lo, 1)

            def step(e, r, known):
                more = known is None or known + 1 < E2

                def gate(c):
                    s = slice(c * CAP, (c + 1) * CAP)
                    dve.wait_ge(silu3, e * NI + c + 1)
                    if known != 0 and c == 0:
                        dve.wait_ge(hid3_lo, e * NI)
                    dve.tensor_tensor(gu[:, s], s_sb[:, s], psG[c][:, CAP:2 * CAP], ALU.mult).then_inc(hid3, 1)

                def low(c):
                    s = slice(c * CAP, (c + 1) * CAP)
                    dve.wait_ge(hid3_hi, e * NI + c + 1)
                    dve.tensor_tensor(hid[:, r, 1, s], gu[:, s], as_f32(hid[:, r, 0, s]), ALU.subtract).then_inc(hid3_lo, 1)
                if more:
                    split(e + 2, 1, r)
                gate(0)
                split(e + 1, 2, 1 - r)
                low(0)
                gate(1)
                low(1)
                gate(2)
                if more:
                    gathered(e + 1)
                low(2)
                if known is None or known + 3 <= E2:
                    split(e + 3, 0, 1 - r)
                if known == 0:
                    dve.wait_ge(r2_wsrc, 1)
                    link(dve.tensor_copy(U[0], psG[3][:, 0:NQ]))
                    link(dve.tensor_tensor(U[1], psG[3][:, NQ:2 * NQ], U[0], ALU.add))
                    dve.tensor_tensor(w_slot[:, :], psG[3][:, 2 * NQ:3 * NQ], U[1], ALU.add).then_inc(r2_w, 1)
            gathered(0)
            weigh(0)
            weigh(1)
            split(2, 0, 0)
            stage3(dve, step)

        @block.tensor
        def _(pe):
            def product(ps, left, right, n, total):
                for m, (a, b) in enumerate(((0, 0), (0, 1), (1, 0))):
                    ins = pe.matmul(ps, left[a], right[b], start=n == 0 and m == 0, stop=n == total - 1 and m == 2)
                return ins

            def transpose4(ps, src):
                for k in range(KD):
                    ins = pe.transpose(ps[:, k * P:(k + 1) * P], src[:, k * P:(k + 1) * P], ident)
                return ins

            pe.wait_ge(in_const, 16)
            pe.wait_ge(r1_tot, 1)
            pe.matmul(psY[0][:, 0:E1], tri, S12(small)[:, 0:E1], start=True, stop=True)
            pe.matmul(psY[0][:, E1:2 * E1], ones, S12(small)[:, 0:E1], start=True, stop=True).then_inc(r1_pre, 1)
            pe.wait_ge(r1_hot, 1)
            for j in range(NJ):
                ins = pe.matmul(psY[1][:, 0:2 * NT], onehot[0][:, j, :], q_tok[0][:, j, 0:2 * NT], start=j == 0, stop=j == NJ - 1)
            ins.then_inc(r1_src, 1)
            pe.wait_ge(r1_idx, 1)
            pe.nop(nofuse=True)

            def weights(t):
                return pe.value_load(tile_e[0:1, bass.ds(t, 1)], min_val=0, max_val=E1 - 1)

            def ctx(w, k):
                return [c[:, bass.ds(w * (KD * D) + k * D, D)] for c in (ctx_hi, ctx_lo)]

            def step(t, par, known):
                if have(known, 0):
                    w = weights(t)
                    pe.wait_ge(ctx_lo_done, pe.snap(w + 1))
                if have(known, -1):
                    pe.wait_ge(gu_ready, t)
                    transpose4(psT[1], gu[:, 0:D]).then_inc(gT_ps, 1)
                if have(known, 0):
                    pe.wait_ge(hT_lo, t + 1)
                    for k in range(KD):
                        s = slice(k * P, (k + 1) * P)
                        ins = product(psG[0][:, :], [hT[0][:, s], hT[1][:, s]], ctx(w, k), k, KD)
                    ins.then_inc(p_ps, 1)
                if have(known, 1):
                    pe.wait_ge(h_ready, t + 2)
                    transpose4(psT[0], h[:, (par + 1) % 2, :]).then_inc(hT_ps, 1)
                if have(known, -1):
                    v = weights(t - 1)
                    pe.wait_ge(gT_lo, t)
                    if have(known, -2):
                        pe.wait_ge(x1_ready, t - 1)
                    for k in range(KD):
                        s = slice(k * P, (k + 1) * P)
                        ins = product(psY[0][:, :], [gT[0][:, s], gT[1][:, s]], ctx(v, k), k, KD)
                    ins.then_inc(y_ps, 1)
            stage1(pe, step)

            def transposed(j):
                pe.wait_ge(ht_here[j % 4], 16 * (j // 4 + 1))
                if j >= 2:
                    pe.wait_ge(bT_lo, j - 1)
                else:
                    pe.wait_ge(gT_lo, NT)
                transpose4(psT[j % 2], ht[:, j % 4, :]).then_inc(bT_ps, 1)

            def up(n):
                b, c = SEQ[n]
                pe.wait_ge(bT_lo, TB * (b + 1))
                if n >= 2:
                    pe.wait_ge(hid_ready, n - 1)
                if n >= 2 and SEQ[n - 2][1] == 2:
                    pe.wait_ge(log_copied, SEQ[n - 2][0] + 1)
                for m in range(2):
                    pe.wait_ge(w_lo[m], 1)
                    for k in range(KD):
                        o = k * IP + c * P
                        left = [piece(s, m)[:, o:o + P] for s in SLOT[0]]
                        ins = product(psG[2 * (n % 2) + m][:, :], left, [part[:, k, :] for part in bl[b % 2]], k, KD)
                    if m == 0 and n in LOG_AT:
                        a = LOG_AT.index(n)
                        pe.wait_ge(log_copied, a + 1)
                        if a:
                            pe.wait_ge(log_ready, a)
                        if a >= 2:
                            pe.wait_ge(y2_copied, TB * 2)
                        for j in range(TB):
                            s = slice(j * P, (j + 1) * P)
                            t = pe.transpose(psY[1][:, s], log_sb[:, s], ident)
                        t.then_inc(log_ps, 1)
                ins.then_inc(up_ps, 1)

            def down(j):
                b = j // TB
                if j % TB == 0:
                    pe.wait_ge(hid_lo, seq_end(b))
                    pe.wait_ge(w_lo[2], 1)
                if j % 2:
                    pe.wait_ge(log_ready, min(2 * (b // 2 + 1), NB))
                if j >= 2:
                    pe.wait_ge(y2_copied, j - 1)
                for c in range(NI):
                    o = c * BT + (j % TB) * P
                    left = [hid[:, b % 2, m, o:o + P] for m in range(2)]
                    right = [piece(s, 2)[:, c * D:(c + 1) * D] for s in SLOT[0]]
                    ins = product(psY[j % 2][:, :], left, right, c, NI)
                ins.then_inc(y2_ps, 1)

            for j in range(TB):
                transposed(j)
            for b in range(2):
                for i in range(NI):
                    up(NI * b + i)
                    if i < 2:
                        for j in (TB * (b + 1) + 2 * i, TB * (b + 1) + 2 * i + 1):
                            transposed(j)
            for j in range(TB * (NB - 1), NJ):
                down(j - 3 * TB)
                transposed(j)
            for j in range(TB, 2 * TB):
                down(j)
            for n in range(2 * NI, NB * NI):
                up(n)
            pe.wait_ge(r2_tot, 1)
            pe.matmul(psT[0][:, 0:E2], tri, small[:, 4 * NJ:5 * NJ], start=True, stop=True).then_inc(r2_pre, 1)

            def to_slots(k, ps, q, ready, n):
                pe.wait_ge(ready, k + 1)
                for j in range(NJ):
                    ins = pe.matmul(ps[:, 0:n], onehot[k][:, j, :], q[k][:, j, :],
                                    start=k == 0 and j == 0, stop=k == 1 and j == NJ - 1)
                return ins

            for j in range(TB * (NB - 2), NJ - 2):
                down(j)
            to_slots(0, psT[1], q_tok, r2_hot, 2 * NQ)
            down(NJ - 2)
            to_slots(1, psT[1], q_tok, r2_hot, 2 * NQ).then_inc(r2_src, 1)
            down(NJ - 1)

            def gathered(e, r, first):
                for a in range(NA):
                    n = 2 * r + a
                    pe.wait_ge(g_here[n], landed(e, r))
                    if not first:
                        pe.wait_ge(g_lo, (e - 1) * NA + a + 1)
                    transpose4(psT[a], ht[:, n, :]).then_inc(g_ps, 1)

            def down3(e, r, first):
                pe.wait_ge(hid3_lo, (e + 1) * NI)
                pe.wait_ge(w_lo[2], e + 2)
                for a in range(NA):
                    if not first:
                        pe.wait_ge(y3_ready, (e - 1) * NA + a + 1)
                    for c in range(NI):
                        o = c * CAP + a * P
                        left = [hid[:, 1 - r, m, o:o + P] for m in range(2)]
                        right = [piece(s, 2)[:, c * D:(c + 1) * D] for s in SLOT[r]]
                        ins = product(psY[a][:, :], left, right, c, NI)
                    ins.then_inc(y3_ps, 1)

            def step(e, r, known):
                pe.wait_ge(g_lo, (e + 1) * NA)
                for m in range(2):
                    pe.wait_ge(w_lo[m], e + 2)
                for c in range(NI):
                    if known != 0:
                        pe.wait_ge(hid3, (e - 1) * NI + c + 1)
                    for m in range(2):
                        for k in range(KD):
                            o = k * IP + c * P
                            left = [piece(s, m)[:, o:o + P] for s in SLOT[1 - r]]
                            ins = product(psG[c][:, m * CAP:(m + 1) * CAP], left,
                                          [part[:, k, 0:CAP] for part in bl[0]], k, KD)
                    ins.then_inc(up3_ps, 1)
                if known is None or known + 1 < E2:
                    gathered(e + 1, 1 - r, False)
                if known == 0:
                    to_slots(0, psG[3], q_w, r2_whot, 3 * NQ)
                    to_slots(1, psG[3], q_w, r2_whot, 3 * NQ).then_inc(r2_wsrc, 1)
                if known is None or known > 0:
                    down3(e - 1, r, known == 1)
            gathered(0, 0, True)
            stage3(pe, step)
            down3(E2 - 1, 1 - (E2 - 1) % 2, False)


SEQ = [(b, c) for b in range(NB - 2) for c in (2, 0, 1)] + [
    (NB - 2, 2), (NB - 1, 2), (NB - 2, 0), (NB - 2, 1), (NB - 1, 0), (NB - 1, 1)]
LOG_AT = [SEQ.index((b, 2)) + 1 for b in range(NB)]


def seq_end(b):
    return 1 + max(n for n, (a, _) in enumerate(SEQ) if a == b)


def S12(small):
    return small[:, 12 * NJ:13 * NJ]


def kernel(**inputs):
    import concourse.bacc as bacc
    from concourse.bass_utils import run_bass_kernel_spmd

    f = {k: np.asarray(v) for k, v in inputs.items()}

    def side(w):
        e = w.shape[0]
        t = np.zeros((e, P, KD, IP), w.dtype)
        t[:, :, :, :I_MLP] = w.reshape(e, I_MLP, KD, P).transpose(0, 3, 2, 1)
        return t

    def down(w):
        e = w.shape[0]
        t = np.zeros((e, IP, D), w.dtype)
        t[:, :I_MLP, :] = w.transpose(0, 2, 1)
        return t.reshape(e, NI, P, D).transpose(0, 2, 1, 3).reshape(e, P, NI * D)

    w1 = side(np.concatenate([f["L0_ffn_Ws1"][None], f["L0_ffn_W1"]]))
    w3 = side(np.concatenate([f["L0_ffn_Ws3"][None], f["L0_ffn_W3"]]))
    w1[0, :, :, I_MLP:I_MLP + E2] = f["L0_ffn_gate_w"].reshape(E2, KD, P).transpose(2, 1, 0)
    arrays = {
        "x": f["x"].reshape(TOK, D),
        "ids": f["itok_BxS_13_99985"].reshape(P, NJ),
        "ctx_t": f["ctx_2048"].reshape(E1, D, KD, P).transpose(0, 3, 2, 1).reshape(E1, P, KD * D),
        "gates": np.broadcast_to(np.concatenate([f["g_xattn"], f["g_ffn"]])[None, :], (P, 2)),
        "w13": np.stack([w1, w3], 2).reshape(E2 + 1, P, 2, KD * IP),
        "w2": down(np.concatenate([f["L0_ffn_Ws2"][None], f["L0_ffn_W2"]])),
        "gate_b": np.broadcast_to(f["L0_ffn_gate_b"][None, :], (P, E2)),
        "const": constants(),
    }
    arrays = {"in_" + k: np.ascontiguousarray(v) for k, v in arrays.items()}
    nc = bacc.Bacc("TRN2", target_bir_lowering=False, num_devices=1)
    args = [nc.dram_tensor(k, v.shape, mybir.dt.from_np(v.dtype), kind="ExternalInput").ap() for k, v in arrays.items()]
    args.append(nc.dram_tensor("out", (TOK + CAP, D), F32, kind="ExternalOutput").ap())
    gated_layer(nc, *args)
    r = run_bass_kernel_spmd(nc, [arrays], core_ids=[0])
    return np.asarray(r.results[0]["out"])[:TOK].reshape(f["x"].shape)
```
